# Optimizing a Trainium2 kernel written in Bass

```python
import numpy as np
import jax
import jax.numpy as jnp

def _softmax(x, axis=-1):
    return jax.nn.softmax(x, axis=axis)
def _gelu(x):
    return jax.nn.gelu(x, approximate=True)
def _silu(x):
    return jax.nn.silu(x)
def _sigmoid(x):
    return jax.nn.sigmoid(x)
def _layernorm(x, axis=-1, eps=1e-5):
    m = jnp.mean(x, axis=axis, keepdims=True)
    v = jnp.var(x, axis=axis, keepdims=True)
    return (x - m) / jnp.sqrt(v + eps)
def _scatter_add(tgt, idx, src, axis=0):
    return tgt.at[idx].add(src)
def _segment_sum(src, seg, n):
    return jax.ops.segment_sum(src, seg, n)

kernel_name = 'mk_metaformer_d2_conv_nchw128_1a2163'

def setup_inputs(seed: int = 0):
    np.random.seed(seed)
    _w = jnp.asarray
    def _rec_inputs():
        import jax
        import jax.numpy as jnp
        _gk = jax.random.key(seed)
        x = -0.0005207 + 1.001 * jax.random.normal(jax.random.fold_in(_gk, 1), (4, 128, 64, 64), jnp.float32)
        return x
    x = _rec_inputs()
    def _L0_conv_setup():
        import jax, jax.numpy as jnp
        import numpy as np
        D_CONV = 4
        D_STATE = 16
        GROUP = 8

        def _ln(x, g, b):
            mu = x.mean(-1, keepdims=True)
            v = ((x - mu) ** 2).mean(-1, keepdims=True)
            return (x - mu) * jax.lax.rsqrt(v + 1e-05) * g + b

        def _mamba(x, W_in, conv_w, conv_b, W_x, W_dt, b_dt, A_log, D_skip, W_out):
            B, L, Dm = x.shape
            d_inner = W_in.shape[0] // 2
            dt_rank = W_dt.shape[1]
            xz = x @ W_in.T
            xi, z = (xz[..., :d_inner], xz[..., d_inner:])
            xc = jax.lax.conv_general_dilated(xi.transpose(0, 2, 1), conv_w, (1,), [(D_CONV - 1, 0)], feature_group_count=d_inner, dimension_numbers=('NCH', 'OIH', 'NCH'))
            u = jax.nn.silu((xc + conv_b[:, None]).transpose(0, 2, 1))
            x_dbl = u @ W_x.T
            dt = jax.nn.softplus(x_dbl[..., :dt_rank] @ W_dt.T + b_dt)
            Bs = x_dbl[..., dt_rank:dt_rank + D_STATE]
            Cs = x_dbl[..., dt_rank + D_STATE:]
            A = -jnp.exp(A_log)

            def step(h, inp):
                dt_t, B_t, C_t, u_t = inp
                dA = jnp.exp(dt_t[..., None] * A)
                h = dA * h + (dt_t * u_t)[..., None] * B_t[:, None, :]
                return (h, jnp.einsum('bdn,bn->bd', h, C_t))
            h0 = jnp.zeros((B, d_inner, D_STATE), x.dtype)
            _, ys = jax.lax.scan(step, h0, (dt.transpose(1, 0, 2), Bs.transpose(1, 0, 2), Cs.transpose(1, 0, 2), u.transpose(1, 0, 2)))
            y = ys.transpose(1, 0, 2) + u * D_skip
            return y * jax.nn.silu(z) @ W_out.T
        key = jax.random.key(seed)
        ks = jax.random.split(key, 10)
        B, C, W, H = (4, 128, 64, 64)
        out_dim = 128
        d_inner = 2 * C
        dt_rank = (C + 15) // 16
        f = lambda k, s, sc=0.02: jax.random.normal(k, s, jnp.float32) * sc
        A_log = jnp.log(jnp.tile(jnp.arange(1, D_STATE + 1, dtype=jnp.float32), (d_inner, 1)))
        return dict(x=jax.random.normal(ks[0], (B, C, W, H), jnp.float32), gamma=jnp.ones((C,), jnp.float32), beta=jnp.zeros((C,), jnp.float32), W_in=f(ks[1], (2 * d_inner, C)), conv_w=f(ks[2], (d_inner, 1, D_CONV), 0.1), conv_b=jnp.zeros((d_inner,), jnp.float32), W_x=f(ks[3], (dt_rank + 2 * D_STATE, d_inner)), W_dt=f(ks[4], (d_inner, dt_rank), 0.1), b_dt=f(ks[5], (d_inner,), 0.5), A_log=A_log, D_skip=jnp.ones((d_inner,), jnp.float32), W_out=f(ks[6], (C, d_inner)), W_p=f(ks[7], (out_dim, C)), b_p=jnp.zeros((out_dim,), jnp.float32), s1=jnp.ones((1,), jnp.float32), s2=jnp.ones((1,), jnp.float32))
    _L0_conv_all = _L0_conv_setup()
    _L0_conv_in = {k: v for k, v in _L0_conv_all.items() if k in ('gamma', 'beta', 'W_in', 'conv_w', 'conv_b', 'W_x', 'W_dt', 'b_dt', 'A_log', 'D_skip', 'W_out', 'W_p', 'b_p', 's1', 's2', )}
    del _L0_conv_all

    def _L0_ffn_setup():
        import jax, jax.numpy as jnp
        import numpy as np
        B, N, D, C, E, K = (8, 8192, 128, 128, 8, 2)
        key = jax.random.key(seed)
        k0, k1, k2 = jax.random.split(key, 3)
        x = jax.random.normal(k0, (B, N, D), dtype=jnp.float32)
        router_w = jax.random.normal(k1, (D, E), dtype=jnp.float32) * 0.05
        router_b = jnp.zeros((E,), dtype=jnp.float32)
        expert_w = jax.random.normal(k2, (E, D, C), dtype=jnp.float32) * (1.0 / np.sqrt(D))
        expert_b = jnp.zeros((E, C), dtype=jnp.float32)
        return {'x': x, 'router_w': router_w, 'router_b': router_b, 'expert_w': expert_w, 'expert_b': expert_b}
    _L0_ffn_all = _L0_ffn_setup()
    _L0_ffn_in = {k: v for k, v in _L0_ffn_all.items() if k in ('router_w', 'router_b', 'expert_w', 'expert_b', )}
    del _L0_ffn_all

    def _L1_conv_setup():
        import jax, jax.numpy as jnp
        import numpy as np
        import math
        from jax import lax
        C = 128
        K = 9
        PAD = K // 2

        def conv1d(x, w, b):
            y = lax.conv_general_dilated(x, w, window_strides=(1,), padding=[(PAD, PAD)], dimension_numbers=('NCH', 'OIH', 'NCH'))
            return y + b[None, :, None]

        def _scan_fwd(slices, w, b):

            def step(carry, s):
                new = s + jax.nn.relu(conv1d(carry, w, b))
                return (new, new)
            _, out = lax.scan(step, slices[0], slices[1:])
            return jnp.concatenate([slices[:1], out], axis=0)

        def _scan_bwd(slices, w, b):

            def step(carry, s):
                new = s + jax.nn.relu(conv1d(carry, w, b))
                return (new, new)
            seg = jnp.flip(slices[1:-1], axis=0)
            _, out = lax.scan(step, slices[-1], seg)
            return jnp.concatenate([slices[:1], jnp.flip(out, axis=0), slices[-1:]], axis=0)
        key = jax.random.key(seed)
        ks = jax.random.split(key, 9)
        B, H, W = (64, 36, 100)
        bound = math.sqrt(2.0 / (C * K * 5))
        bias_bound = 1.0 / math.sqrt(C * K)
        x = jax.random.normal(ks[0], (B, C, H, W), dtype=jnp.float32)

        def wgt(k):
            return jax.random.uniform(k, (C, C, K), dtype=jnp.float32, minval=-bound, maxval=bound)

        def bia(k):
            return jax.random.uniform(k, (C,), dtype=jnp.float32, minval=-bias_bound, maxval=bias_bound)
        return {'x': x, 'w_d': wgt(ks[1]), 'b_d': bia(ks[2]), 'w_u': wgt(ks[3]), 'b_u': bia(ks[4]), 'w_r': wgt(ks[5]), 'b_r': bia(ks[6]), 'w_l': wgt(ks[7]), 'b_l': bia(ks[8])}
    _L1_conv_all = _L1_conv_setup()
    _L1_conv_in = {k: v for k, v in _L1_conv_all.items() if k in ('w_d', 'b_d', 'w_u', 'b_u', 'w_r', 'b_r', 'w_l', 'b_l', )}
    del _L1_conv_all

    def _L1_ffn_setup():
        import jax, jax.numpy as jnp
        import numpy as np
        PADDED_SL = 8192
        TEMPERATURE = 1.0
        SIGMA_POW = 0.25

        def _stu_conv(phi, u, n):
            b, sl, d = u.shape
            sgn = jnp.where(jnp.arange(sl) % 2 == 0, 1.0, -1.0).astype(u.dtype)
            sgn3 = sgn[None, :, None]
            Vf = jnp.fft.rfft(phi, n=n, axis=0)
            Uf_p = jnp.fft.rfft(u, n=n, axis=1)
            Uf_m = jnp.fft.rfft(u * sgn3, n=n, axis=1)
            U_plus = jnp.fft.irfft(Vf[None, :, :, None] * Uf_p[:, :, None, :], n=n, axis=1)[:, :sl]
            U_minus = jnp.fft.irfft(Vf[None, :, :, None] * Uf_m[:, :, None, :], n=n, axis=1)[:, :sl]
            U_minus = U_minus * sgn[None, :, None, None]
            return (U_plus, U_minus)

        def _compute_spectral(u, sigma, phi, Mpp, Mpm):
            U_plus, U_minus = _stu_conv(phi, u, PADDED_SL)
            s = sigma ** SIGMA_POW
            out = jnp.einsum('btkd,k,kde->bte', U_plus, s, Mpp)
            out = out + jnp.einsum('btkd,k,kde->bte', U_minus, s, Mpm)
            return out

        def _compute_ar_u(Mu, u):
            sl = u.shape[1]
            out = jnp.zeros(u.shape[:2] + (Mu.shape[-1],), dtype=u.dtype)
            for i in range(Mu.shape[0]):
                ui = jnp.pad(u, ((0, 0), (i, 0), (0, 0)))[:, :sl]
                out = out + jnp.einsum('btd,de->bte', ui, Mu[i])
            return out

        def _stu(u, sigma, phi, Mu, Mpp, Mpm):
            return _compute_spectral(u, sigma, phi, Mpp, Mpm) + _compute_ar_u(Mu, u)
        key = jax.random.key(seed)
        ks = jax.random.split(key, 8)
        b, sl, d, K, k_u = (2, 4096, 128, 16, 3)
        x = jax.random.normal(ks[0], (b, sl, d), dtype=jnp.float32)
        sigma = jax.random.uniform(ks[1], (K,), dtype=jnp.float32, minval=0.001, maxval=1.0)
        phi = jax.random.normal(ks[2], (sl, K), dtype=jnp.float32) / np.sqrt(sl)
        M_u = jax.random.normal(ks[3], (4, k_u, d, d), dtype=jnp.float32) * 0.02
        M_phi_plus = jax.random.normal(ks[4], (4, K, d, d), dtype=jnp.float32) * 0.02
        M_phi_minus = jax.random.normal(ks[5], (4, K, d, d), dtype=jnp.float32) * 0.02
        log_weights = jnp.ones((4,), dtype=jnp.float32)
        u01 = jax.random.uniform(ks[6], (4,), dtype=jnp.float32, minval=1e-06, maxval=1.0 - 1e-06)
        gumbel = -jnp.log(-jnp.log(u01))
        return {'x': x, 'sigma': sigma, 'phi': phi, 'M_u': M_u, 'M_phi_plus': M_phi_plus, 'M_phi_minus': M_phi_minus, 'log_weights': log_weights, 'gumbel': gumbel}
    _L1_ffn_all = _L1_ffn_setup()
    _L1_ffn_in = {k: v for k, v in _L1_ffn_all.items() if k in ('sigma', 'phi', 'M_u', 'M_phi_plus', 'M_phi_minus', 'log_weights', 'gumbel', )}
    del _L1_ffn_all

    return {
        "x": x,
        "L0_conv_gamma": _L0_conv_in["gamma"],
        "L0_conv_beta": _L0_conv_in["beta"],
        "L0_conv_W_in": _L0_conv_in["W_in"],
        "L0_conv_conv_w": _L0_conv_in["conv_w"],
        "L0_conv_conv_b": _L0_conv_in["conv_b"],
        "L0_conv_W_x": _L0_conv_in["W_x"],
        "L0_conv_W_dt": _L0_conv_in["W_dt"],
        "L0_conv_b_dt": _L0_conv_in["b_dt"],
        "L0_conv_A_log": _L0_conv_in["A_log"],
        "L0_conv_D_skip": _L0_conv_in["D_skip"],
        "L0_conv_W_out": _L0_conv_in["W_out"],
        "L0_conv_W_p": _L0_conv_in["W_p"],
        "L0_conv_b_p": _L0_conv_in["b_p"],
        "L0_conv_s1": _L0_conv_in["s1"],
        "L0_conv_s2": _L0_conv_in["s2"],
        "L0_ffn_router_w": _L0_ffn_in["router_w"],
        "L0_ffn_router_b": _L0_ffn_in["router_b"],
        "L0_ffn_expert_w": _L0_ffn_in["expert_w"],
        "L0_ffn_expert_b": _L0_ffn_in["expert_b"],
        "L1_conv_w_d": _L1_conv_in["w_d"],
        "L1_conv_b_d": _L1_conv_in["b_d"],
        "L1_conv_w_u": _L1_conv_in["w_u"],
        "L1_conv_b_u": _L1_conv_in["b_u"],
        "L1_conv_w_r": _L1_conv_in["w_r"],
        "L1_conv_b_r": _L1_conv_in["b_r"],
        "L1_conv_w_l": _L1_conv_in["w_l"],
        "L1_conv_b_l": _L1_conv_in["b_l"],
        "L1_ffn_sigma": _L1_ffn_in["sigma"],
        "L1_ffn_phi": _L1_ffn_in["phi"],
        "L1_ffn_M_u": _L1_ffn_in["M_u"],
        "L1_ffn_M_phi_plus": _L1_ffn_in["M_phi_plus"],
        "L1_ffn_M_phi_minus": _L1_ffn_in["M_phi_minus"],
        "L1_ffn_log_weights": _L1_ffn_in["log_weights"],
        "L1_ffn_gumbel": _L1_ffn_in["gumbel"],
    }

def reference(x, L0_conv_gamma, L0_conv_beta, L0_conv_W_in, L0_conv_conv_w, L0_conv_conv_b, L0_conv_W_x, L0_conv_W_dt, L0_conv_b_dt, L0_conv_A_log, L0_conv_D_skip, L0_conv_W_out, L0_conv_W_p, L0_conv_b_p, L0_conv_s1, L0_conv_s2, L0_ffn_router_w, L0_ffn_router_b, L0_ffn_expert_w, L0_ffn_expert_b, L1_conv_w_d, L1_conv_b_d, L1_conv_w_u, L1_conv_b_u, L1_conv_w_r, L1_conv_b_r, L1_conv_w_l, L1_conv_b_l, L1_ffn_sigma, L1_ffn_phi, L1_ffn_M_u, L1_ffn_M_phi_plus, L1_ffn_M_phi_minus, L1_ffn_log_weights, L1_ffn_gumbel):
    import jax
    import jax.numpy as jnp
    def _L0_conv_ref(x, gamma, beta, W_in, conv_w, conv_b, W_x, W_dt, b_dt, A_log, D_skip, W_out, W_p, b_p, s1, s2):
        import jax, jax.numpy as jnp
        import numpy as np
        D_CONV = 4
        D_STATE = 16
        GROUP = 8

        def _ln(x, g, b):
            mu = x.mean(-1, keepdims=True)
            v = ((x - mu) ** 2).mean(-1, keepdims=True)
            return (x - mu) * jax.lax.rsqrt(v + 1e-05) * g + b

        def _mamba(x, W_in, conv_w, conv_b, W_x, W_dt, b_dt, A_log, D_skip, W_out):
            B, L, Dm = x.shape
            d_inner = W_in.shape[0] // 2
            dt_rank = W_dt.shape[1]
            xz = x @ W_in.T
            xi, z = (xz[..., :d_inner], xz[..., d_inner:])
            xc = jax.lax.conv_general_dilated(xi.transpose(0, 2, 1), conv_w, (1,), [(D_CONV - 1, 0)], feature_group_count=d_inner, dimension_numbers=('NCH', 'OIH', 'NCH'))
            u = jax.nn.silu((xc + conv_b[:, None]).transpose(0, 2, 1))
            x_dbl = u @ W_x.T
            dt = jax.nn.softplus(x_dbl[..., :dt_rank] @ W_dt.T + b_dt)
            Bs = x_dbl[..., dt_rank:dt_rank + D_STATE]
            Cs = x_dbl[..., dt_rank + D_STATE:]
            A = -jnp.exp(A_log)

            def step(h, inp):
                dt_t, B_t, C_t, u_t = inp
                dA = jnp.exp(dt_t[..., None] * A)
                h = dA * h + (dt_t * u_t)[..., None] * B_t[:, None, :]
                return (h, jnp.einsum('bdn,bn->bd', h, C_t))
            h0 = jnp.zeros((B, d_inner, D_STATE), x.dtype)
            _, ys = jax.lax.scan(step, h0, (dt.transpose(1, 0, 2), Bs.transpose(1, 0, 2), Cs.transpose(1, 0, 2), u.transpose(1, 0, 2)))
            y = ys.transpose(1, 0, 2) + u * D_skip
            return y * jax.nn.silu(z) @ W_out.T
        B, C, W, H = x.shape
        L = W * H
        x_flat = x.reshape(B, C, L).transpose(0, 2, 1)
        x1 = _ln(x_flat, gamma, beta)
        cpg = C // GROUP
        x2 = x.reshape(B, GROUP, cpg, W, H).transpose(0, 2, 1, 3, 4).reshape(B, C, L).transpose(0, 2, 1)
        x2 = _ln(x2, gamma, beta)
        m = lambda t: _mamba(t, W_in, conv_w, conv_b, W_x, W_dt, b_dt, A_log, D_skip, W_out)
        xm = m(x1) + x1 * s1 + (m(x2) + x2 * s2)
        xm = _ln(xm, gamma, beta)
        out = xm @ W_p.T + b_p
        return out.transpose(0, 2, 1).reshape(B, -1, W, H)

    def _L0_ffn_ref(x, router_w, router_b, expert_w, expert_b):
        import jax, jax.numpy as jnp
        import numpy as np
        B, N, D, C, E, K = (8, 8192, 128, 128, 8, 2)
        router_probs = jax.nn.softmax(x @ router_w + router_b, axis=-1)
        top_p, top_i = jax.lax.top_k(router_probs, K)
        top_p = top_p / jnp.sum(top_p, axis=-1, keepdims=True)
        expert_out = jnp.einsum('bnd,edc->bnec', x, expert_w) + expert_b
        gathered = jnp.take_along_axis(expert_out, top_i[..., None], axis=2)
        return jnp.einsum('bnk,bnkc->bnc', top_p, gathered)

    def _L1_conv_ref(x, w_d, b_d, w_u, b_u, w_r, b_r, w_l, b_l):
        import jax, jax.numpy as jnp
        import numpy as np
        import math
        from jax import lax
        C = 128
        K = 9
        PAD = K // 2

        def conv1d(x, w, b):
            y = lax.conv_general_dilated(x, w, window_strides=(1,), padding=[(PAD, PAD)], dimension_numbers=('NCH', 'OIH', 'NCH'))
            return y + b[None, :, None]

        def _scan_fwd(slices, w, b):

            def step(carry, s):
                new = s + jax.nn.relu(conv1d(carry, w, b))
                return (new, new)
            _, out = lax.scan(step, slices[0], slices[1:])
            return jnp.concatenate([slices[:1], out], axis=0)

        def _scan_bwd(slices, w, b):

            def step(carry, s):
                new = s + jax.nn.relu(conv1d(carry, w, b))
                return (new, new)
            seg = jnp.flip(slices[1:-1], axis=0)
            _, out = lax.scan(step, slices[-1], seg)
            return jnp.concatenate([slices[:1], jnp.flip(out, axis=0), slices[-1:]], axis=0)
        rows = jnp.moveaxis(x, 2, 0)
        rows = _scan_fwd(rows, w_d, b_d)
        rows = _scan_bwd(rows, w_u, b_u)
        y = jnp.moveaxis(rows, 0, 2)
        cols = jnp.moveaxis(y, 3, 0)
        cols = _scan_fwd(cols, w_r, b_r)
        cols = _scan_bwd(cols, w_l, b_l)
        return jnp.moveaxis(cols, 0, 3)

    def _L1_ffn_ref(x, sigma, phi, M_u, M_phi_plus, M_phi_minus, log_weights, gumbel):
        import jax, jax.numpy as jnp
        import numpy as np
        PADDED_SL = 8192
        TEMPERATURE = 1.0
        SIGMA_POW = 0.25

        def _stu_conv(phi, u, n):
            b, sl, d = u.shape
            sgn = jnp.where(jnp.arange(sl) % 2 == 0, 1.0, -1.0).astype(u.dtype)
            sgn3 = sgn[None, :, None]
            Vf = jnp.fft.rfft(phi, n=n, axis=0)
            Uf_p = jnp.fft.rfft(u, n=n, axis=1)
            Uf_m = jnp.fft.rfft(u * sgn3, n=n, axis=1)
            U_plus = jnp.fft.irfft(Vf[None, :, :, None] * Uf_p[:, :, None, :], n=n, axis=1)[:, :sl]
            U_minus = jnp.fft.irfft(Vf[None, :, :, None] * Uf_m[:, :, None, :], n=n, axis=1)[:, :sl]
            U_minus = U_minus * sgn[None, :, None, None]
            return (U_plus, U_minus)

        def _compute_spectral(u, sigma, phi, Mpp, Mpm):
            U_plus, U_minus = _stu_conv(phi, u, PADDED_SL)
            s = sigma ** SIGMA_POW
            out = jnp.einsum('btkd,k,kde->bte', U_plus, s, Mpp)
            out = out + jnp.einsum('btkd,k,kde->bte', U_minus, s, Mpm)
            return out

        def _compute_ar_u(Mu, u):
            sl = u.shape[1]
            out = jnp.zeros(u.shape[:2] + (Mu.shape[-1],), dtype=u.dtype)
            for i in range(Mu.shape[0]):
                ui = jnp.pad(u, ((0, 0), (i, 0), (0, 0)))[:, :sl]
                out = out + jnp.einsum('btd,de->bte', ui, Mu[i])
            return out

        def _stu(u, sigma, phi, Mu, Mpp, Mpm):
            return _compute_spectral(u, sigma, phi, Mpp, Mpm) + _compute_ar_u(Mu, u)
        T = x.shape[1]
        outs = []
        for i, frac in enumerate((1, 2, 4, 8)):
            xi = x[:, :T // frac]
            si = _stu(xi, sigma, phi, M_u[i], M_phi_plus[i], M_phi_minus[i])
            si = jnp.pad(si, ((0, 0), (0, T - si.shape[1]), (0, 0)))
            outs.append(si)
        y_soft = jax.nn.softmax((log_weights + gumbel) / TEMPERATURE)
        y_hard = jax.nn.one_hot(jnp.argmax(y_soft), 4, dtype=y_soft.dtype)
        weights = y_hard - jax.lax.stop_gradient(y_soft) + y_soft
        stacked = jnp.stack(outs, axis=-1)
        return jnp.sum(stacked * weights, axis=-1)

    def _gn(v, G=32, eps=1e-5):
        B_, C_, H_, W_ = v.shape
        g = v.reshape(B_, G, C_ // G, H_, W_)
        m = jnp.mean(g, axis=(2, 3, 4), keepdims=True)
        s = jnp.var(g, axis=(2, 3, 4), keepdims=True)
        return ((g - m) / jnp.sqrt(s + eps)).reshape(v.shape)

    def _ln_c(v, eps=1e-6):
        m = jnp.mean(v, axis=1, keepdims=True)
        s = jnp.var(v, axis=1, keepdims=True)
        return (v - m) / jnp.sqrt(s + eps)

    def _ln_t(v, eps=1e-5):
        m = jnp.mean(v, axis=-1, keepdims=True)
        s = jnp.var(v, axis=-1, keepdims=True)
        return (v - m) / jnp.sqrt(s + eps)

    def _to_tokens(v):
        B_, C_, H_, W_ = v.shape
        return v.reshape(B_, C_, H_ * W_).transpose(0, 2, 1)
    def _from_tokens(t, like):
        B_, C_, H_, W_ = like.shape
        return t.transpose(0, 2, 1).reshape(B_, C_, H_, W_)

    x = x + _L0_conv_ref(_ln_c(x), L0_conv_gamma, L0_conv_beta, L0_conv_W_in, L0_conv_conv_w, L0_conv_conv_b, L0_conv_W_x, L0_conv_W_dt, L0_conv_b_dt, L0_conv_A_log, L0_conv_D_skip, L0_conv_W_out, L0_conv_W_p, L0_conv_b_p, L0_conv_s1, L0_conv_s2)
    t = _to_tokens(x)
    t = t + _L0_ffn_ref(_ln_t(t), L0_ffn_router_w, L0_ffn_router_b, L0_ffn_expert_w, L0_ffn_expert_b)
    x = _from_tokens(t, x)
    x = x + _L1_conv_ref(_ln_c(x), L1_conv_w_d, L1_conv_b_d, L1_conv_w_u, L1_conv_b_u, L1_conv_w_r, L1_conv_b_r, L1_conv_w_l, L1_conv_b_l)
    t = _to_tokens(x)
    t = t + _L1_ffn_ref(_ln_t(t), L1_ffn_sigma, L1_ffn_phi, L1_ffn_M_u, L1_ffn_M_phi_plus, L1_ffn_M_phi_minus, L1_ffn_log_weights, L1_ffn_gumbel)
    x = _from_tokens(t, x)
    return x


_drawn_inputs = setup_inputs


def setup_inputs(seed=0):
    import zlib

    import numpy as np

    out = dict(_drawn_inputs(seed))
    spreads = {'L0_conv_gamma': (1.0, 0.2),
     'L0_conv_beta': (0.0, 0.1),
     'L0_conv_conv_b': (0.0, 0.714),
     'L0_conv_D_skip': (1.0, 0.6),
     'L0_conv_b_p': (0.0, 0.1),
     'L0_ffn_router_b': (0.0, 0.1),
     'L0_ffn_expert_b': (0.0, 0.1),
     'L1_ffn_log_weights': (1.0, 0.2)}
    factors = {'L0_conv_W_in': 5.009,
     'L0_conv_conv_w': 6.578,
     'L0_conv_W_x': 8.0,
     'L0_conv_W_dt': 8.0,
     'L0_conv_b_dt': 8.0,
     'L0_conv_A_log': 8.0,
     'L0_conv_W_out': 4.978,
     'L1_conv_b_d': 8.0,
     'L1_conv_b_u': 8.0,
     'L1_conv_b_r': 8.0,
     'L1_conv_b_l': 8.0}
    for name, (base, spread) in spreads.items():
        noise = np.random.default_rng([zlib.crc32(name.encode()), seed]).standard_normal(out[name].shape)
        drawn = base * np.exp(spread * noise) if base else spread * noise
        out[name] = jnp.asarray(drawn.astype(out[name].dtype))
    for name, factor in factors.items():
        out[name] = (out[name] * factor).astype(out[name].dtype)
    return out
```

```python
from contextlib import ExitStack

import concourse.bass as bass
from concourse import mybir

F32 = mybir.dt.float32
F32R = mybir.dt.float32r
BF16 = mybir.dt.bfloat16
U32 = mybir.dt.uint32
ALU = mybir.AluOpType
ACT = mybir.ActivationFunctionType
AX = mybir.AxisListType

C = 128
IMG = 4
LEN = 4096
TOK = IMG * LEN
SIDE = 64
NT = 512
QUAD = 4 * NT


class Scope:

    def __init__(self, nc, ctx, tag):
        self.nc, self.ctx, self.tag = nc, ctx, tag

    def sb(self, name, shape, dt=F32):
        return self.ctx.enter_context(self.nc.sbuf_tensor(f"{self.tag}_{name}", shape, dt))

    def ps(self, name, shape, dt=F32):
        return self.ctx.enter_context(self.nc.psum_tensor(f"{self.tag}_{name}", shape, dt))

    def sem(self, name):
        return self.ctx.enter_context(self.nc.semaphore(f"{self.tag}_{name}"))


def load_stage(nc, tag, pairs):
    with ExitStack() as ctx:
        s = Scope(nc, ctx, tag)
        moved = s.sem("moved")
        block = ctx.enter_context(nc.Block())

        @block.sync
        def _(sp):
            for dst, src in pairs:
                sp.dma_start(dst, src).then_inc(moved, 16)
            sp.wait_ge(moved, 16 * len(pairs))


def layernorm_stage(nc, tag, consts, src, dst, eps, gamma=None):
    with ExitStack() as ctx:
        s = Scope(nc, ctx, tag)
        square = s.sb("square", [C, 4, NT])
        deviation = s.sb("deviation", [C, 4, 4])
        rstd = s.sb("rstd", [C, 4, 4])
        eps_col = s.sb("eps", [C, 1])
        bank = s.ps("bank", [C, 4, NT])
        var_bank = s.ps("var", [C, 4, NT])
        mean_ready = s.sem("mean_ready")
        eps_set = s.sem("eps_set")
        centred = s.sem("centred")
        squared = s.sem("squared")
        var_ready = s.sem("var_ready")
        std_ready = s.sem("std_ready")
        rstd_ready = s.sem("rstd_ready")
        spread = s.sem("spread")
        normed = s.sem("normed")
        block = ctx.enter_context(nc.Block())
        steps = TOK // QUAD

        @block.tensor
        def _(pe):
            with pe.Fori(0, steps) as i:
                for t in range(4):
                    pe.wait_ge(normed, 4 * i + t + 1)
                    nc.tensor.matmul(bank[:, t], consts["mean"][:], src[:, bass.ds(i * QUAD + t * NT, NT)],
                                     start=True, stop=True).then_inc(mean_ready, 1)
                for t in range(4):
                    pe.wait_ge(squared, 4 * i + t + 1)
                    pe.wait_ge(std_ready, 4 * i + t + 1)
                    for k in range(4):
                        mm = nc.tensor.matmul(var_bank[:, t, k:k + 1],
                                              square[:, t, 128 * k:128 * k + 128], consts["mean"][:, 0:1],
                                              start=True, stop=True)
                    mm.then_inc(var_ready, 1)
                for t in range(4):
                    pe.wait_ge(rstd_ready, 4 * i + t + 1)
                    for k in range(4):
                        mm = nc.tensor.matmul(bank[:, t, 128 * k:128 * k + 128],
                                              rstd[:, t, k:k + 1].to_broadcast([C, C]), consts["ident"][:],
                                              start=True, stop=True)
                    mm.then_inc(spread, 1)

        @block.scalar
        def _(act):
            act.wait_ge(eps_set, 1)
            with act.Fori(0, steps) as i:
                for t in range(4):
                    act.wait_ge(centred, 4 * i + t + 1)
                    nc.scalar.activation(square[:, t], dst[:, bass.ds(i * QUAD + t * NT, NT)],
                                         ACT.Square).then_inc(squared, 1)
                for t in range(4):
                    act.wait_ge(var_ready, 4 * i + t + 1)
                    nc.scalar.activation(deviation[:, t], var_bank[:, t, 0:4], ACT.Sqrt,
                                         bias=eps_col[:, 0:1]).then_inc(std_ready, 1)

        @block.vector
        def _(dve):
            nc.vector.memset(eps_col[:], eps).then_inc(eps_set, 1)
            dve.sem_inc(normed, 4)
            dve.sem_inc(std_ready, 4)
            with dve.Fori(0, steps) as i:
                for t in range(4):
                    dve.wait_ge(mean_ready, 4 * i + t + 1)
                    cols = bass.ds(i * QUAD + t * NT, NT)
                    nc.vector.tensor_tensor(dst[:, cols], src[:, cols], bank[:, t], ALU.subtract).then_inc(centred, 1)
                for t in range(4):
                    dve.wait_ge(std_ready, 4 * i + t + 5)
                    nc.vector.reciprocal(rstd[:, t], deviation[:, t]).then_inc(rstd_ready, 1)
                for t in range(4):
                    dve.wait_ge(spread, 4 * i + t + 1)
                    tile = dst[:, bass.ds(i * QUAD + t * NT, NT)]
                    if gamma is None:
                        nc.vector.tensor_tensor(tile, tile, bank[:, t], ALU.mult).then_inc(normed, 1)
                    else:
                        nc.vector.scalar_tensor_tensor(out=tile, in0=tile, scalar=gamma, in1=bank[:, t],
                                                       op0=ALU.mult, op1=ALU.mult).then_inc(normed, 1)


INNER = 2 * C
STATES = 16
TAPS = 4
HIST = TAPS - 1
PAIRS = TOK // (2 * NT)
COLUMNS = (("gamma", 0, 1), ("beta", 1, 1), ("conv_b", 2, 2), ("b_dt", 4, 2), ("d", 6, 2), ("s", 8, 2))
PAD = NT


def mamba_stage(nc, tag, consts, w, xh):
    with ExitStack() as ctx:
        s = Scope(nc, ctx, tag)
        x_in = s.sb("x_in", [C, 2, 2, HIST + NT])
        u = s.sb("u", [C, 2, 2, NT])
        gate = s.sb("gate", [C, 2, 2, NT])
        dt = s.sb("dt", [C, 2, 2, NT])
        dtu = s.sb("dtu", [C, 2, 2, NT])
        x_dbl = s.sb("x_dbl", [C, NT])
        bc_high = s.sb("bc_high", [96, NT], BF16)
        bc_rest = s.sb("bc_rest", [96, NT])
        bc_mid = s.sb("bc_mid", [96, NT], BF16)
        bc = s.sb("bc", [96, 2, NT], BF16)
        soft_abs = s.sb("soft_abs", [C, 2, NT])
        soft_pos = s.sb("soft_pos", [C, 2, NT])
        soft_ln = s.sb("soft_ln", [C, 2, NT])
        decay = s.sb("decay", [C, 4, 2, NT])
        inject = s.sb("inject", [C, 2, 2, NT])
        h = s.sb("h", [C, 4, 2, NT])
        hc = s.sb("hc", [C, 2, 2, NT])
        carry = s.sb("carry", [C, 2, STATES, 2])
        y1 = s.sb("y1", [C, 2, NT])
        y2 = s.sb("y2", [C, 2, NT])
        skip = s.sb("skip", [C, 2, NT])
        zero = s.sb("zero", [C, 1])
        conv_in = w["conv_w"]
        neg_a = w["a_log"]
        front = s.ps("front", [C, 2, NT])
        b_bank = s.ps("b_bank", [C, 2, NT])
        c_bank = s.ps("c_bank", [C, 2, NT])
        y_bank = s.ps("y_bank", [C, 2, NT])

        fronted = s.sem("fronted")
        front_step = s.sem("front_step")
        hist_ready = s.sem("hist_ready")
        rounded = s.sem("rounded")
        dt_part = s.sem("dt_part")
        rest_ready = s.sem("rest_ready")
        mid_ready = s.sem("mid_ready")
        bc_ready = s.sem("bc_ready")
        dt_ready = s.sem("dt_ready")
        dtu_ready = s.sem("dtu_ready")
        b_ready = s.sem("b_ready")
        c_ready = s.sem("c_ready")
        summed = s.sem("summed")
        decayed = s.sem("decayed")
        injected = s.sem("injected")
        scanned = s.sem("scanned")
        carried = s.sem("carried")
        weighed = s.sem("weighed")
        y1_ready = s.sem("y1_ready")
        y2_ready = s.sem("y2_ready")
        out_ready = s.sem("out_ready")
        skip_ready = s.sem("skip_ready")
        stored = s.sem("stored")
        masked = s.sem("masked")
        zeroed = s.sem("zeroed")
        prepared = s.sem("prepared")
        a_ready = s.sem("a_ready")
        block = ctx.enter_context(nc.Block())

        def tile_cols(i, tile):
            return bass.ds(i * (2 * NT) + (PAD + tile * NT), NT)

        @block.tensor
        def _(pe):
            def front_order(i, U, q, first=False):
                if not first:
                    pe.wait_ge(front_step, 13 * U - 2)
                nc.tensor.matmul(front[:, 0], w["order"][:, q % 2], xh[:, tile_cols(i, q // 2)],
                                 start=True, stop=True).then_inc(fronted, 1)

            def front_in(U, q, first=False):
                pe.wait_ge(front_step, 13 * U + 1)
                pe.wait_ge(hist_ready, U + 1)
                if not first:
                    pe.wait_ge(skip_ready, U)
                for half in range(2):
                    for j in range(TAPS):
                        mm = nc.tensor.matmul(front[:, half], conv_in[:, j, half * C:(half + 1) * C],
                                              x_in[:, q % 2, q // 2, j:j + NT],
                                              start=(j == 0), stop=(j == TAPS - 1))
                    mm.then_inc(fronted, 1)
                for half in range(2):
                    pe.wait_ge(front_step, 13 * U + 2 + half)
                    nc.tensor.matmul(front[:, half], w["in"][:, INNER + half * C:INNER + (half + 1) * C],
                                     x_in[:, q % 2, q // 2, HIST:HIST + NT],
                                     start=True, stop=True).then_inc(fronted, 1)

            def front_x(U, q):
                pe.wait_ge(front_step, 13 * U + 4)
                nc.tensor.matmul(front[:, 0], w["x"][:, 0], u[:, q % 2, 0], start=True, stop=False)
                nc.tensor.matmul(front[:, 0], w["x"][:, 1], u[:, q % 2, 1], start=False,
                                 stop=True).then_inc(fronted, 1)

            def front_dt(U):
                pe.wait_ge(front_step, 13 * U + 6)
                nc.tensor.matmul(front[:, 1], w["dt"][:, 0:C], x_dbl[:], start=True, stop=True).then_inc(fronted, 1)
                pe.wait_ge(front_step, 13 * U + 7)
                nc.tensor.matmul(front[:, 0], w["dt"][:, C:INNER], x_dbl[:], start=True, stop=True).then_inc(fronted, 1)

            def out_proj(U):
                pe.wait_ge(y2_ready, U + 2)
                pe.wait_ge(front_step, 13 * U + 9)
                nc.tensor.matmul(front[:, 1], w["out"][:, 0], y2[:, 0], start=True, stop=False)
                nc.tensor.matmul(front[:, 1], w["out"][:, 1], y2[:, 1], start=False,
                                 stop=True).then_inc(out_ready, 1)

            def spread_b(g, n, slot):
                pe.wait_ge(injected, g + 1)
                nc.tensor.matmul(b_bank[:, n % 2], w["select"][:, n], bc[:, slot],
                                 start=True, stop=True).then_inc(b_ready, 1)

            def spread_c(g, n, slot):
                pe.wait_ge(weighed, g + 1)
                nc.tensor.matmul(c_bank[:, n % 2], w["select"][:, STATES + n], bc[:, slot],
                                 start=True, stop=True).then_inc(c_ready, 1)

            def add_up(n):
                for half in range(2):
                    mm = nc.tensor.matmul(y_bank[:, half], consts["ident"][:], hc[:, n % 2, half],
                                          start=(n == 0), stop=(n == STATES - 1), skip_group_check=True)
                mm.then_inc(summed, 1)

            pe.wait_ge(zeroed, 1)
            pe.wait_ge(prepared, 1)
            for half in range(2):
                nc.tensor.matmul(y_bank[:, half], consts["ident"][:], hc[:, 0, half], start=True, stop=False,
                                 skip_group_check=True)
            front_order(0, 0, 0, first=True)
            front_in(0, 0, first=True)
            front_x(0, 0)
            front_dt(0)
            with pe.Fori(0, PAIRS) as i:
                for q in range(4):
                    U = 4 * i + q
                    ni, nq = i + (q + 1) // 4, (q + 1) % 4
                    pe.wait_ge(bc_ready, U + 1)
                    for n in range(STATES):
                        g = 16 * U + n
                        spread_b(g, n, q % 2)
                        spread_c(g, (n - 1) % STATES, (q if n else q - 1) % 2)
                        if n == 3:
                            pe.wait_ge(y1_ready, U + 1)
                        add_up((n - 3) % STATES)
                        if n == 4:
                            out_proj(U)
                        if n == 6:
                            front_order(ni, U + 1, nq)
                        if n == 8:
                            front_in(U + 1, nq)
                        if n == 9:
                            front_x(U + 1, nq)
                        if n == 10:
                            front_dt(U + 1)
            U = 4 * PAIRS
            pe.wait_ge(bc_ready, U + 1)
            spread_b(16 * U, 0, 0)
            spread_c(16 * U, STATES - 1, 1)
            for k in range(3):
                pe.wait_ge(weighed, 16 * U + 1 + k)
                add_up(STATES - 3 + k)
            out_proj(U)

        @block.scalar
        def _(act):
            def act_front(U, q, first=False):
                slot = q % 2
                act.wait_ge(fronted, 8 * U + 1)
                act.wait_ge(hist_ready, U + 1)
                if not first:
                    act.wait_ge(skip_ready, U)
                nc.scalar.activation(x_in[:, q % 2, q // 2, HIST:HIST + NT], front[:, 0], ACT.Identity,
                                     bias=w["beta"][:, 0:1], scale=w["gamma"][:, 0:1]).then_inc(front_step, 1)
                if not first:
                    act.wait_ge(y1_ready, U)
                    act.wait_ge(y2_ready, U + 1)
                for k in range(4):
                    act.wait_ge(fronted, 8 * U + 2 + k)
                    bias = w["conv_b"][:, k:k + 1] if k < 2 else 0.0
                    nc.scalar.activation((u, gate)[k // 2][:, slot, k % 2], front[:, k % 2], ACT.Silu,
                                         bias=bias).then_inc(front_step, 1)
                act.wait_ge(fronted, 8 * U + 6)
                if not first:
                    act.wait_ge(bc_ready, U)
                nc.scalar.activation(x_dbl[:], front[:, 0], ACT.Copy).then_inc(front_step, 1)
                nc.scalar.activation(bc_high[:], front[0:96, 0], ACT.Copy).then_inc(front_step, 1)
                if not first:
                    act.wait_ge(dt_ready, U)
                for half in range(2):
                    act.wait_ge(fronted, 8 * U + 7 + half)
                    bias = w["b_dt"][:, half:half + 1]
                    nc.scalar.activation(soft_abs[:, half], front[:, 1 - half], ACT.Abs,
                                         bias=bias).then_inc(front_step, 1)
                    nc.scalar.activation(soft_pos[:, half], front[:, 1 - half], ACT.Relu,
                                         bias=bias).then_inc(front_step, 1)
                act.wait_ge(front_step, 13 * U + 11)
                nc.scalar.activation(soft_abs[:], soft_abs[:], ACT.Exp, scale=-1.0).then_inc(front_step, 1)
                act.wait_ge(front_step, 13 * U + 12)
                nc.scalar.activation(soft_ln[:], soft_abs[:], ACT.Ln, bias=1.0).then_inc(front_step, 1)

            nc.scalar.activation(neg_a[:], neg_a[:], ACT.Exp).then_inc(a_ready, 1)
            act.wait_ge(zeroed, 1)
            act_front(0, 0, first=True)
            act.wait_ge(prepared, 1)
            with act.Fori(0, PAIRS) as i:
                for q in range(4):
                    U = 4 * i + q
                    act.wait_ge(dt_ready, U + 1)
                    for n in range(STATES):
                        g = 16 * U + n
                        act.wait_ge(scanned, g + 1)
                        for half in range(2):
                            e = nc.scalar.activation(decay[:, n % 4, half], dt[:, q % 2, half], ACT.Exp,
                                                     scale=neg_a[:, half, n:n + 1])
                        e.then_inc(decayed, 1)
                        if n == 10:
                            act_front(U + 1, (q + 1) % 4)

        @block.vector
        def _(dve):
            def history(i, U, q, first=False):
                dst = x_in[:, q % 2, q // 2, 0:HIST]
                src = x_in[:, q % 2, 1 - q // 2, NT:NT + HIST]
                if first:
                    nc.vector.memset(dst, 0.0).then_inc(hist_ready, 1)
                    return
                dve.wait_ge(front_step, 13 * (U - 1) + 1)
                if q // 2:
                    nc.vector.tensor_copy(dst, src).then_inc(hist_ready, 1)
                else:
                    nc.vector.tensor_scalar(dst, src, w["mask"][:, bass.ds(i, 1)], None,
                                            ALU.mult).then_inc(hist_ready, 1)

            def round_trip(U, q):
                dve.wait_ge(front_step, 13 * U + 12)
                nc.vector.tensor_scalar(dt[:, q % 2], soft_abs[:], 1.0, 1.0, ALU.add,
                                        ALU.subtract).then_inc(rounded, 1)

            def rest(U):
                dve.wait_ge(front_step, 13 * U + 7)
                nc.vector.scalar_tensor_tensor(out=bc_rest[:], in0=bc_high[:], scalar=w["less"][:, 0:1],
                                               in1=x_dbl[0:96, :], op0=ALU.mult, op1=ALU.add).then_inc(rest_ready, 1)

            def parts(U, q, first=False):
                dve.wait_ge(mid_ready, U + 1)
                if not first:
                    dve.wait_ge(c_ready, 16 * U - 15)
                nc.vector.scalar_tensor_tensor(out=bc[:, q % 2], in0=bc_mid[:], scalar=w["less"][:, 1:2],
                                               in1=bc_rest[:], op0=ALU.mult, op1=ALU.add).then_inc(bc_ready, 1)

            def do_inject(g, n, slot):
                dve.wait_ge(b_ready, g + 1)
                dve.wait_ge(scanned, g + 3)
                nc.vector.tensor_tensor(inject[:, n % 2], dtu[:, slot],
                                        b_bank[:, n % 2].unsqueeze(1).to_broadcast([C, 2, NT]),
                                        ALU.mult).then_inc(injected, 1)

            def do_scan(g, n, v):
                dve.wait_ge(decayed, g + 1)
                dve.wait_ge(injected, g + 3)
                dve.wait_ge(carried, g + 1)
                dve.wait_ge(weighed, g + 1)
                for half in range(2):
                    sc = nc.vector.tensor_tensor_scan(h[:, n % 4, half], decay[:, n % 4, half],
                                                      inject[:, n % 2, half], carry[:, v, n, half:half + 1],
                                                      ALU.mult, ALU.add)
                sc.then_inc(scanned, 1)

            def do_weigh(g, n):
                dve.wait_ge(c_ready, g + 1)
                dve.wait_ge(summed, g + 1)
                dve.wait_ge(scanned, g + 4)
                nc.vector.tensor_tensor(hc[:, n % 2], h[:, n % 4],
                                        c_bank[:, n % 2].unsqueeze(1).to_broadcast([C, 2, NT]),
                                        ALU.mult).then_inc(weighed, 1)

            def end_y(U, q):
                dve.wait_ge(summed, 16 * U + 3)
                dve.wait_ge(y2_ready, U + 1)
                for half in range(2):
                    y = nc.vector.scalar_tensor_tensor(out=y1[:, half], in0=u[:, (q - 1) % 2, half],
                                                       scalar=w["d"][:, half:half + 1], in1=y_bank[:, half],
                                                       op0=ALU.mult, op1=ALU.add)
                y.then_inc(y1_ready, 1)

            def end_skip(i, U, q):
                v, p = (q - 1) % 2, ((q - 1) // 2) % 2
                dve.wait_ge(out_ready, U + 2)
                if v == 0:
                    dve.wait_ge(stored, 2 * i + q // 2 + 1)
                nc.vector.scalar_tensor_tensor(out=skip[:, v], in0=x_in[:, v, p, HIST:HIST + NT],
                                               scalar=w["s"][:, v:v + 1], in1=front[:, 1],
                                               op0=ALU.mult, op1=ALU.add).then_inc(skip_ready, 1)

            for half in range(2):
                for j in range(TAPS):
                    cols = slice(half * C, (half + 1) * C)
                    nc.vector.tensor_tensor(conv_in[:, j, cols], conv_in[:, j, cols], w["in"][:, cols], ALU.mult)
            dve.wait_ge(a_ready, 1)
            nc.vector.tensor_scalar(neg_a[:], neg_a[:], -1.0, None, ALU.mult).then_inc(prepared, 1)
            for z in (x_in, hc, h, u, gate, carry, bc, zero):
                nc.vector.memset(z[:], 0.0)
            nc.vector.memset(xh[:, 0:PAD], 0.0)
            nc.vector.memset(xh[:, PAD + TOK:], 0.0).then_inc(zeroed, 1)
            dve.wait_ge(zeroed, 1)
            dve.sem_inc(injected, 2)
            dve.sem_inc(scanned, 4)
            dve.sem_inc(weighed, 2)
            history(0, 0, 0, first=True)
            rest(0)
            round_trip(0, 0)
            parts(0, 0, first=True)
            dve.wait_ge(dtu_ready, 1)
            do_inject(0, 0, 0)
            with dve.Fori(0, PAIRS) as i:
                for q in range(4):
                    U = 4 * i + q
                    ni, nq = i + (q + 1) // 4, (q + 1) % 4
                    if q < 2:
                        dve.wait_ge(carried, 16 * U + 1)
                        dve.wait_ge(scanned, 16 * U + 4)
                        nc.vector.tensor_scalar(carry[:, q % 2], carry[:, q % 2], w["mask"][:, bass.ds(i, 1)],
                                                None, ALU.mult).then_inc(masked, 1)
                        dve.wait_ge(masked, 2 * i + q + 1)
                    for n in range(STATES):
                        g = 16 * U + n
                        if n == 3:
                            end_y(U, q)
                        do_scan(g, n, q % 2)
                        if n == STATES - 1:
                            dve.wait_ge(dtu_ready, U + 2)
                        do_inject(g + 1, (n + 1) % STATES, (q if n < STATES - 1 else q + 1) % 2)
                        do_weigh(g, (n - 1) % STATES)
                        if n == 1:
                            history(ni, U + 1, nq)
                        if n == 6:
                            end_skip(i, U, q)
                        if n == 11:
                            rest(U + 1)
                        if n == 12:
                            round_trip(U + 1, nq)
                        if n == 13:
                            parts(U + 1, nq)
            U = 4 * PAIRS
            do_weigh(16 * U, STATES - 1)
            end_y(U, 0)
            end_skip(PAIRS, U, 0)

        @block.gpsimd
        def _(pool):
            def middle(U):
                pool.wait_ge(rest_ready, U + 1)
                nc.gpsimd.tensor_tensor(bc_mid[:], bc_rest[:], zero[0:96].to_broadcast([96, NT]),
                                        ALU.add).then_inc(mid_ready, 1)

            def steps_dt(U, q, first=False):
                slot = dt[:, q % 2]
                pool.wait_ge(rounded, U + 1)
                nc.gpsimd.tensor_tensor(slot, soft_abs[:], slot, ALU.subtract).then_inc(dt_part, 1)
                pool.wait_ge(front_step, 13 * U + 13)
                pool.wait_ge(dt_part, 2 * U + 1)
                nc.gpsimd.tensor_tensor(slot, soft_ln[:], slot, ALU.add).then_inc(dt_part, 1)
                pool.wait_ge(dt_part, 2 * U + 2)
                nc.gpsimd.tensor_tensor(slot, soft_pos[:], slot, ALU.add).then_inc(dt_ready, 1)
                pool.wait_ge(dt_ready, U + 1)
                if not first:
                    pool.wait_ge(injected, 16 * U - 14)
                nc.gpsimd.tensor_tensor(dtu[:, q % 2], dt[:, q % 2], u[:, q % 2], ALU.mult).then_inc(dtu_ready, 1)

            def keep(g, n, v):
                pool.wait_ge(scanned, g + 5)
                last = h[:, n % 4, :, NT - 1]
                nc.gpsimd.tensor_tensor(carry[:, v, n], last, zero[:].to_broadcast([C, 2]), ALU.add).then_inc(carried, 1)

            def end_gate(U, q):
                pool.wait_ge(y1_ready, U + 1)
                pool.wait_ge(out_ready, U + 1)
                nc.gpsimd.tensor_tensor(y2[:], y1[:], gate[:, (q - 1) % 2], ALU.mult).then_inc(y2_ready, 1)

            def store(i, U, q):
                pool.wait_ge(skip_ready, U + 1)
                nc.gpsimd.tensor_tensor(xh[:, tile_cols(i, q // 2 - 1)], skip[:, 0], skip[:, 1],
                                        ALU.add).then_inc(stored, 1)

            pool.wait_ge(zeroed, 1)
            nc.gpsimd.memset(skip[:], 0.0)
            pool.sem_inc(carried, 2)
            pool.sem_inc(y2_ready, 1)
            pool.sem_inc(out_ready, 1)
            middle(0)
            steps_dt(0, 0, first=True)
            with pool.Fori(0, PAIRS) as i:
                for q in range(4):
                    U = 4 * i + q
                    for n in range(STATES):
                        keep(16 * U + n, n, q % 2)
                        if n == 3:
                            end_gate(U, q)
                        if n == 6 and q % 2 == 0:
                            store(i, U, q)
                        if n == 12:
                            middle(U + 1)
                            steps_dt(U + 1, (q + 1) % 4)
            U = 4 * PAIRS
            end_gate(U, 0)
            store(PAIRS, U, 0)


def project_stage(nc, tag, w, src, x):
    with ExitStack() as ctx:
        s = Scope(nc, ctx, tag)
        bank = s.ps("bank", [C, 4, NT])
        bias = s.sb("bias", [C, 1])
        projected = s.sem("projected")
        beta_ready = s.sem("beta_ready")
        bias_ready = s.sem("bias_ready")
        added = s.sem("added")
        block = ctx.enter_context(nc.Block())

        @block.tensor
        def _(pe):
            nc.tensor.matmul(bank[:, 0, 0:1], w["w_p"][:], w["beta"][:], start=True, stop=True).then_inc(beta_ready, 1)
            pe.wait_ge(bias_ready, 1)
            with pe.Fori(0, TOK // QUAD) as i:
                for t in range(4):
                    pe.wait_ge(added, 4 * i + t + 1)
                    nc.tensor.matmul(bank[:, t], w["w_p"][:], src[:, bass.ds(i * QUAD + t * NT, NT)],
                                     start=True, stop=True).then_inc(projected, 1)

        @block.vector
        def _(dve):
            dve.sem_inc(added, 4)
            dve.wait_ge(beta_ready, 1)
            nc.vector.tensor_tensor(bias[:], bank[:, 0, 0:1], w["b_p"][:], ALU.add).then_inc(bias_ready, 1)
            dve.wait_ge(bias_ready, 1)
            with dve.Fori(0, TOK // QUAD) as i:
                for t in range(4):
                    dve.wait_ge(projected, 4 * i + t + 1)
                    tile = x[:, bass.ds(i * QUAD + t * NT, NT)]
                    nc.vector.scalar_tensor_tensor(out=tile, in0=bank[:, t], scalar=bias[:, 0:1], in1=tile,
                                                   op0=ALU.add, op1=ALU.add).then_inc(added, 1)


EXPERTS = 8
SUB = NT // 128


def experts_stage(nc, tag, consts, w, xn, x):
    with ExitStack() as ctx:
        s = Scope(nc, ctx, tag)
        x_tile = s.sb("x_tile", [C, 2, NT])
        logits = s.sb("logits", [C, SUB, EXPERTS])
        best = s.sb("best", [C, SUB, 8])
        best_at = s.sb("best_at", [C, SUB, 8], U32)
        at = s.sb("at", [C, SUB, 2])
        gap = s.sb("gap", [C, SUB])
        ratio = s.sb("ratio", [C, SUB])
        denom = s.sb("denom", [C, SUB])
        share = s.sb("share", [C, SUB, 2])
        hot = s.sb("hot", [C, 2, SUB, EXPERTS])
        gates = s.sb("gates", [C, 2, SUB, EXPERTS])
        gates_t = s.sb("gates_t", [EXPERTS, NT])
        scaled = s.sb("scaled", [C, 2, EXPERTS, C])
        mixed = s.sb("mixed", [C, SUB, C])
        logit_bank = s.ps("logit_bank", [C, NT])
        expert_bank = s.ps("expert_bank", [C, 2, EXPERTS, C])
        gate_bank = s.ps("gate_bank", [C, NT])
        out_bank = s.ps("out_bank", [C, NT])
        copied = s.sem("copied")
        routed = s.sem("routed")
        step = s.sem("step")
        ratio_ready = s.sem("ratio_ready")
        turned = s.sem("turned")
        gates_ready = s.sem("gates_ready")
        expert_ready = s.sem("expert_ready")
        scaled_ready = s.sem("scaled_ready")
        mixed_ready = s.sem("mixed_ready")
        back = s.sem("back")
        added = s.sem("added")
        block = ctx.enter_context(nc.Block())
        TILES = TOK // NT
        ROUTER = 19

        @block.tensor
        def _(pe):
            def route(j, slot):
                pe.wait_ge(copied, j + 1)
                for k in range(SUB):
                    mm = nc.tensor.matmul(logit_bank[:, EXPERTS * k:EXPERTS * (k + 1)],
                                          x_tile[:, slot, 128 * k:128 * (k + 1)], w["router"][:],
                                          start=True, stop=True)
                mm.then_inc(routed, 1)

            def turn_back(j, slot, k):
                pe.wait_ge(mixed_ready, SUB * j + k + 1)
                nc.tensor.matmul(out_bank[:, 128 * k:128 * (k + 1)], mixed[:, k], consts["ident"][:],
                                 start=True, stop=False)
                nc.tensor.matmul(out_bank[:, 128 * k:128 * (k + 1)], w["bias"][:],
                                 gates_t[:, 128 * k:128 * (k + 1)], start=False, stop=True).then_inc(back, 1)

            route(0, 0)
            with pe.Fori(0, TILES // 2) as i:
                for slot in range(2):
                    j = 2 * i + slot
                    pe.wait_ge(step, ROUTER * (j + 1))
                    for k in range(SUB):
                        mm = nc.tensor.matmul(gate_bank[0:EXPERTS, 128 * k:128 * (k + 1)],
                                              gates[:, slot, k], consts["ident"][:], start=True, stop=True)
                    mm.then_inc(turned, 1)
                    route(j + 1, 1 - slot)
                    for k in range(SUB):
                        pe.wait_ge(scaled_ready, SUB * j + k + 1)
                        for part in range(2):
                            mm = nc.tensor.matmul(expert_bank[:, k % 2, 4 * part:4 * (part + 1)],
                                                  x_tile[:, slot, 128 * k:128 * (k + 1)],
                                                  w["expert"][:, 4 * part:4 * (part + 1)], start=True, stop=True)
                        mm.then_inc(expert_ready, 1)
                        if k == 1:
                            pe.wait_ge(gates_ready, j + 1)
                            pe.wait_ge(added, j + 1)
                        if k:
                            turn_back(j, slot, k - 1)
                    turn_back(j, slot, SUB - 1)

        @block.scalar
        def _(act):
            def copy(i, slot):
                nc.scalar.activation(x_tile[:, slot], xn[:, bass.ds(i * 2 * NT + slot * NT, NT)],
                                     ACT.Copy).then_inc(copied, 1)

            def ratios(j):
                act.wait_ge(step, ROUTER * j + 10)
                nc.scalar.activation(ratio[:], gap[:], ACT.Exp).then_inc(ratio_ready, 1)

            copy(0, 0)
            ratios(0)
            with act.Fori(0, TILES // 2) as i:
                for slot in range(2):
                    j = 2 * i + slot
                    act.wait_ge(turned, j + 1)
                    copy(i + slot, 1 - slot)
                    nc.scalar.activation(gates_t[:], gate_bank[0:EXPERTS, :], ACT.Copy).then_inc(gates_ready, 1)
                    ratios(j + 1)

        @block.vector
        def _(dve):
            def router(j, slot, part, first=False):
                done = ROUTER * j
                lanes = [C, SUB, EXPERTS]
                if part == 0:
                    dve.wait_ge(routed, j + 1)
                    nc.vector.tensor_tensor(logits[:].rearrange("p k e -> p (k e)"), logit_bank[:, 0:SUB * EXPERTS],
                                            w["router_b"][:].rearrange("p k e -> p (k e)"), ALU.add).then_inc(step, 1)
                if part == 1:
                    if first:
                        dve.wait_ge(step, done + 1)
                    for k in range(SUB):
                        nc.vector.max(out=best[:, k], in_=logits[:, k]).then_inc(step, 1)
                    dve.wait_ge(step, done + 5)
                    nc.vector.tensor_tensor(gap[:], best[:, :, 1], best[:, :, 0], ALU.subtract).then_inc(step, 1)
                    for k in range(SUB):
                        nc.vector.max_index(out=best_at[:, k], in_max=best[:, k], in_values=logits[:, k]).then_inc(step, 1)
                if part == 2:
                    dve.wait_ge(step, done + 10)
                    nc.vector.tensor_copy(at[:], best_at[:, :, 0:2]).then_inc(step, 1)
                    dve.wait_ge(ratio_ready, j + 1)
                    nc.vector.tensor_scalar(denom[:], ratio[:], 1.0, None, ALU.add).then_inc(step, 1)
                    dve.wait_ge(step, done + 12)
                    nc.vector.reciprocal(share[:, :, 0], denom[:]).then_inc(step, 1)
                    for r in range(2):
                        nc.vector.tensor_tensor(hot[:, r], w["index"][:].unsqueeze(1).to_broadcast(lanes),
                                                at[:, :, r:r + 1].to_broadcast(lanes), ALU.is_equal).then_inc(step, 1)
                    dve.wait_ge(step, done + 13)
                    nc.vector.tensor_tensor(share[:, :, 1], ratio[:], share[:, :, 0], ALU.mult).then_inc(step, 1)
                if part == 3:
                    dve.wait_ge(step, done + 16)
                    for r in range(2):
                        nc.vector.tensor_tensor(hot[:, r], hot[:, r], share[:, :, r:r + 1].to_broadcast(lanes),
                                                ALU.mult).then_inc(step, 1)
                    dve.wait_ge(step, done + 18)
                    nc.vector.tensor_tensor(gates[:, slot], hot[:, 0], hot[:, 1], ALU.add).then_inc(step, 1)

            dve.sem_inc(scaled_ready, 2)
            dve.sem_inc(added, 1)
            for part in range(4):
                router(0, 0, part, first=True)
            with dve.Fori(0, TILES // 2) as i:
                for slot in range(2):
                    j = 2 * i + slot
                    dve.wait_ge(step, ROUTER * (j + 1))
                    for k in range(SUB):
                        dve.wait_ge(expert_ready, SUB * j + k + 1)
                        if k == 1:
                            dve.wait_ge(step, ROUTER * (j + 1) + 1)
                        nc.vector.tensor_tensor(scaled[:, k % 2], expert_bank[:, k % 2],
                                                gates[:, slot, k].unsqueeze(2).to_broadcast([C, EXPERTS, C]),
                                                ALU.mult).then_inc(scaled_ready, 1)
                        router(j + 1, 1 - slot, k)
                        dve.wait_ge(scaled_ready, SUB * j + k + 3)
                        if k == 0:
                            dve.wait_ge(added, j + 1)
                        nc.vector.tensor_reduce(mixed[:, k], scaled[:, k % 2].rearrange("p e c -> p c e"), AX.X,
                                                ALU.add).then_inc(mixed_ready, 1)
                    dve.wait_ge(back, SUB * (j + 1))
                    tile = x[:, bass.ds(i * 2 * NT + slot * NT, NT)]
                    nc.vector.tensor_tensor(tile, tile, out_bank[:], ALU.add).then_inc(added, 1)


KERNEL = 9
EDGE = KERNEL // 2
PASSES = (("h", 1), ("h", -1), ("w", 1), ("w", -1))


def sweep_stage(nc, tag, w, a):
    with ExitStack() as ctx:
        s = Scope(nc, ctx, tag)
        run = s.sb("run", [C, 2, IMG, SIDE + 2 * EDGE])
        neg_b = s.sb("neg_b", [C, 4])
        bank = s.ps("bank", [C, 2, NT])
        ready = s.sem("ready")
        convolved = s.sem("convolved")
        placed = s.sem("placed")
        biased = s.sem("biased")
        block = ctx.enter_context(nc.Block())
        view = a.rearrange("c (b h w) -> c b h w", b=IMG, h=SIDE)
        G = IMG // 2

        def slices(axis, at, images=slice(0, IMG)):
            return view[:, images, at, :] if axis == "h" else view[:, images, :, at]

        def line(axis, at, g):
            images = slice(g * G, (g + 1) * G)
            if axis == "h":
                return view[:, images, bass.ds(at, 1), :].rearrange("c b o w -> c b (o w)")
            return view[:, images, :, bass.ds(at, 1)].rearrange("c b h o -> c b (h o)")

        steps = [SIDE - 1 if d > 0 else SIDE - 2 for _, d in PASSES]
        made = [2 * (sum(steps[:k]) + k) for k in range(4)]
        done = [2 * sum(steps[:k]) for k in range(4)]

        def each_step(eng, k, do):
            d = PASSES[k][1]
            first = 1 if d > 0 else SIDE - 2
            with eng.Fori(0, steps[k] // 2) as i:
                for r in range(2):
                    do(2 * i + r, r, 2 * i + (first + r) if d > 0 else i * -2 + (first - r))
            if steps[k] % 2:
                t = steps[k] - 1
                do(t, t % 2, first + d * t)

        @block.tensor
        def _(pe):
            for k in range(4):
                def conv(t, slot, at, k=k):
                    for g in range(2):
                        pe.wait_ge(ready, made[k] + 2 * t + g + 1)
                        for j in range(KERNEL):
                            mm = nc.tensor.matmul(bank[:, g, 0:G * SIDE], w["sweep"][:, k, j],
                                                  run[:, slot, g * G:(g + 1) * G, j:j + SIDE],
                                                  start=(j == 0), stop=(j == KERNEL - 1))
                        mm.then_inc(convolved, 1)

                each_step(pe, k, conv)

        @block.vector
        def _(dve):
            nc.vector.memset(run[:], 0.0).then_inc(biased, 1)
            nc.vector.tensor_scalar(neg_b[:], w["sweep_b"][:], -1.0, None, ALU.mult).then_inc(biased, 1)
            dve.sem_inc(placed, 4)
            for k, (axis, d) in enumerate(PASSES):
                dve.wait_ge(placed, 4 + done[k])
                dve.wait_ge(biased, 2 + k)
                last = SIDE if d > 0 else SIDE - 1
                swept = slices(axis, slice(1, last))
                nc.vector.tensor_scalar(swept, swept, w["sweep_b"][:, k:k + 1], None, ALU.add).then_inc(biased, 1)
                for g in range(2):
                    images = slice(g * G, (g + 1) * G)
                    nc.vector.tensor_copy(run[:, 0, images, EDGE:EDGE + SIDE],
                                          slices(axis, 0 if d > 0 else SIDE - 1, images)).then_inc(ready, 1)
                dve.wait_ge(biased, 3 + k)

                def finish(t, slot, at, k=k, axis=axis):
                    for g in range(2):
                        dve.wait_ge(placed, done[k] + 2 * t + g + 1)
                        dve.wait_ge(convolved, done[k] + 2 * t + g + 1)
                        nc.vector.scalar_tensor_tensor(
                            out=run[:, 1 - slot, g * G:(g + 1) * G, EDGE:EDGE + SIDE],
                            in0=bank[:, g, 0:G * SIDE].rearrange("c (b l) -> c b l", b=G), scalar=neg_b[:, k:k + 1],
                            in1=line(axis, at, g), op0=ALU.max, op1=ALU.add).then_inc(ready, 1)

                each_step(dve, k, finish)

        @block.scalar
        def _(act):
            for k, (axis, d) in enumerate(PASSES):
                def place(t, slot, at, k=k, axis=axis):
                    for g in range(2):
                        act.wait_ge(ready, made[k] + 2 * t + g + 3)
                        nc.scalar.activation(line(axis, at, g), run[:, 1 - slot, g * G:(g + 1) * G, EDGE:EDGE + SIDE],
                                             ACT.Copy).then_inc(placed, 1)

                each_step(act, k, place)


def add_stage(nc, tag, x, y):
    with ExitStack() as ctx:
        s = Scope(nc, ctx, tag)
        added = s.sem("added")
        block = ctx.enter_context(nc.Block())

        @block.vector
        def _(dve):
            nc.vector.tensor_tensor(x, x, y, ALU.add).then_inc(added, 1)
            dve.wait_ge(added, 1)


FILTERS = 16
QS = 2 * FILTERS
BLOCKS = 16
PLANES = 32
FRACS = (1, 2, 4, 8)
GENERATOR = 256
Q4 = 4
GROUPS = QS // Q4


def choice_stage(nc, tag, w):
    with ExitStack() as ctx:
        s = Scope(nc, ctx, tag)
        logit = s.sb("logit", [C, 4])
        top = s.sb("top", [C, 1])
        soft = s.sb("soft", [C, 4])
        total = s.sb("total", [C, 1])
        hard = s.sb("hard", [C, 4])
        left = s.sb("left", [C, 4])
        parts = s.sb("parts", [C, 4])
        root = s.sb("root", [C, FILTERS])
        step = s.sem("step")
        raised = s.sem("raised")
        rooted = s.sem("rooted")
        block = ctx.enter_context(nc.Block())
        weight, segment, sigma4 = w["weight"], w["segment"], w["sigma4"]

        @block.scalar
        def _(act):
            act.wait_ge(step, 3)
            nc.scalar.activation(soft[:], logit[:], ACT.Exp).then_inc(raised, 1)
            nc.scalar.activation(root[:], w["sigma"][:], ACT.Sqrt).then_inc(rooted, 1)
            act.wait_ge(rooted, 1)
            nc.scalar.activation(sigma4[:], root[:], ACT.Sqrt).then_inc(rooted, 1)

        @block.vector
        def _(dve):
            count = 0

            def do(instruction):
                nonlocal count
                count += 1
                instruction.then_inc(step, 1)
                dve.wait_ge(step, count)

            do(nc.vector.tensor_tensor(logit[:], w["log_weights"][:], w["gumbel"][:], ALU.add))
            do(nc.vector.tensor_reduce(top[:], logit[:], AX.X, ALU.max))
            do(nc.vector.tensor_scalar(logit[:], logit[:], top[:, 0:1], None, ALU.subtract))
            dve.wait_ge(raised, 1)
            do(nc.vector.tensor_reduce(total[:], soft[:], AX.X, ALU.add))
            do(nc.vector.reciprocal(total[:], total[:]))
            do(nc.vector.tensor_scalar(soft[:], soft[:], total[:, 0:1], None, ALU.mult))
            do(nc.vector.tensor_reduce(top[:], soft[:], AX.X, ALU.max))
            do(nc.vector.tensor_scalar(hard[:], soft[:], top[:, 0:1], None, ALU.is_ge))
            do(nc.vector.tensor_scalar(parts[:], hard[:], -1.0, 1.0, ALU.mult, ALU.add))
            do(nc.vector.memset(left[:], 1.0))
            for k in range(1, 4):
                do(nc.vector.tensor_tensor(left[:, k:k + 1], left[:, k - 1:k], parts[:, k - 1:k], ALU.mult))
            do(nc.vector.tensor_tensor(hard[:], hard[:], left[:], ALU.mult))
            do(nc.vector.tensor_tensor(weight[:], hard[:], soft[:], ALU.subtract))
            do(nc.vector.tensor_tensor(weight[:], weight[:], soft[:], ALU.add))
            for k in range(4):
                do(nc.vector.tensor_reduce(segment[:, k:k + 1], hard[:, 0:4 - k], AX.X, ALU.add))
            do(nc.vector.tensor_tensor(w["block_mask"][:], w["segment_of"][:], segment[0:64, :], ALU.mult))
            do(nc.vector.tensor_reduce(w["mask_col"][:], w["block_mask"][:], AX.X, ALU.add))
            do(nc.vector.tensor_scalar(w["m_u"][:], w["m_u_all"][:, 0], weight[:, 0:1], None, ALU.mult))
            for k in range(1, 4):
                do(nc.vector.scalar_tensor_tensor(out=w["m_u"][:], in0=w["m_u_all"][:, k], scalar=weight[:, k:k + 1],
                                                  in1=w["m_u"][:], op0=ALU.mult, op1=ALU.add))


def autoregressive_stage(nc, tag, w, u, x):
    TILES = LEN // NT
    with ExitStack() as ctx:
        s = Scope(nc, ctx, tag)
        bank = s.ps("bank", [C, 4, NT])
        summed = s.sem("summed")
        added = s.sem("added")
        block = ctx.enter_context(nc.Block())

        @block.tensor
        def _(pe):
            with pe.Fori(0, IMG) as b:
                for t in range(TILES):
                    pe.wait_ge(added, TILES * b + t + 1)
                    for i in range(3):
                        cut = i if t == 0 else 0
                        mm = nc.tensor.matmul(bank[:, t % 4, cut:NT], w["m_u"][:, i],
                                              u[:, bass.ds(b * LEN + (t * NT - i + cut), NT - cut)],
                                              start=(i == 0), stop=(i == 2), skip_group_check=True)
                    mm.then_inc(summed, 1)

        @block.vector
        def _(dve):
            dve.sem_inc(added, 4)
            with dve.Fori(0, IMG) as b:
                for t in range(TILES):
                    dve.wait_ge(summed, TILES * b + t + 1)
                    tile = x[:, bass.ds(b * LEN + t * NT, NT)]
                    k = (0, 1, 2, 2, 3, 3, 3, 3)[t]
                    nc.vector.scalar_tensor_tensor(out=tile, in0=bank[:, t % 4], scalar=w["segment"][:, k:k + 1],
                                                   in1=tile, op0=ALU.mult, op1=ALU.add).then_inc(added, 1)


def turn_stage(nc, tag, consts, u, x, turned_dram, x_dram):
    with ExitStack() as ctx:
        s = Scope(nc, ctx, tag)
        out = s.sb("out", [C, 4, 4, C])
        staged = s.sb("staged", [C, 4, NT])
        bank = s.ps("bank", [C, 4, 4, C])
        staged_ready = s.sem("staged_ready")
        turned = s.sem("turned")
        copied = s.sem("copied")
        stored = [s.sem(f"stored{t}") for t in range(4)]
        x_stored = s.sem("x_stored")
        block = ctx.enter_context(nc.Block())
        steps = TOK // QUAD

        @block.sync
        def _(sp):
            sp.dma_start(x_dram, x).then_inc(x_stored, 16)
            with sp.Fori(0, steps) as i:
                for t in range(4):
                    sp.wait_ge(copied, 4 * i + t + 5)
                    rows = turned_dram[bass.ds(i * QUAD + t * NT, NT), :].rearrange("(k p) c -> p k c", p=128)
                    sp.dma_start(rows, out[:, t]).then_inc(stored[t], 16)
            for t in range(4):
                sp.wait_ge(stored[t], 16 * (steps + 1))
            sp.wait_ge(x_stored, 16)

        @block.tensor
        def _(pe):
            with pe.Fori(0, steps) as i:
                for t in range(4):
                    pe.wait_ge(staged_ready, 4 * i + t + 1)
                    pe.wait_ge(copied, 4 * i + t + 1)
                    for k in range(4):
                        mm = nc.tensor.matmul(bank[:, t, k], staged[:, t, 128 * k:128 * (k + 1)], consts["ident"][:],
                                              start=True, stop=True)
                    mm.then_inc(turned, 1)

        @block.scalar
        def _(act):
            with act.Fori(0, steps) as i:
                for t in range(4):
                    act.wait_ge(copied, 4 * i + t + 1)
                    nc.scalar.activation(staged[:, t], u[:, bass.ds(i * QUAD + t * NT, NT)],
                                         ACT.Copy).then_inc(staged_ready, 1)

        @block.vector
        def _(dve):
            dve.sem_inc(copied, 4)
            for t in range(4):
                dve.sem_inc(stored[t], 16)
            with dve.Fori(0, steps) as i:
                for t in range(4):
                    dve.wait_ge(turned, 4 * i + t + 1)
                    dve.wait_ge(stored[t], 16 * i + 16)
                    nc.vector.tensor_copy(out[:, t], bank[:, t]).then_inc(copied, 1)


def generator_stage(nc, tag, w, high_dram, low_dram):
    with ExitStack() as ctx:
        s = Scope(nc, ctx, tag)
        taps = s.sb("taps", [BLOCKS, QS, 128])
        high = s.sb("high", [PLANES, QS, GENERATOR], F32R)
        low = s.sb("low", [PLANES, QS, GENERATOR], F32R)
        bank = s.ps("bank", [PLANES, 4, Q4, 128])
        loaded = s.sem("loaded")
        transformed = s.sem("transformed")
        rounded = s.sem("rounded")
        split = s.sem("split")
        stored = s.sem("stored")
        block = ctx.enter_context(nc.Block())
        work = [(g, v) for g in range(GROUPS) for v in range(2)]

        @block.sync
        def _(sp):
            sp.dma_start(taps[:], w["phi"]).then_inc(loaded, 16)
            sp.wait_ge(split, len(work))
            sp.dma_start(high_dram, high[:].bitcast(F32)).then_inc(stored, 16)
            sp.dma_start(low_dram, low[:].bitcast(F32)).then_inc(stored, 16)
            sp.wait_ge(stored, 32)

        @block.tensor
        def _(pe):
            pe.wait_ge(loaded, 16)
            for n, (g, v) in enumerate(work):
                if n >= 4:
                    pe.wait_ge(split, n - 3)
                nc.tensor.matmul(bank[:, n % 4], w["dft_taps"][:, v], taps[:, Q4 * g:Q4 * (g + 1)],
                                 start=True, stop=True).then_inc(transformed, 1)

        @block.vector
        def _(dve):
            for n, (g, v) in enumerate(work):
                part = (slice(None), slice(Q4 * g, Q4 * (g + 1)), slice(128 * v, 128 * (v + 1)))
                dve.wait_ge(transformed, n + 1)
                nc.vector.tensor_copy(high[part], bank[:, n % 4]).then_inc(rounded, 1)
                dve.wait_ge(rounded, n + 1)
                nc.vector.tensor_tensor(low[part], bank[:, n % 4], high[part].bitcast(F32),
                                        ALU.subtract).then_inc(split, 1)


def forward_stage(nc, tag, w, turned_dram, uhat_dram):
    FREE = 32 * C
    with ExitStack() as ctx:
        s = Scope(nc, ctx, tag)
        rows = s.sb("rows", [C, 2, FREE])
        out = s.sb("out", [C, 2, FREE])
        bank = s.ps("bank", [C, 8, NT])
        loaded = [s.sem(f"loaded{k}") for k in range(2)]
        transformed = s.sem("transformed")
        copied_a = s.sem("copied_a")
        copied_d = s.sem("copied_d")
        stored = [s.sem(f"stored{k}") for k in range(2)]
        block = ctx.enter_context(nc.Block())
        src = turned_dram.rearrange("(b p n) c -> p b (n c)", b=IMG, p=128)
        T = FREE // NT

        @block.sync
        def _(sp):
            def load(b):
                sp.dma_start(rows[:, b % 2], src[:, b]).then_inc(loaded[b % 2], 16)

            load(0)
            load(1)
            for n in range(2 * IMG):
                b, half = n // 2, n % 2
                sp.wait_ge(copied_a, T // 2 * (n + 1))
                sp.wait_ge(copied_d, T // 2 * (n + 1))
                dst = uhat_dram[16 * half:16 * (half + 1), :, b].rearrange("p x n c -> p x (n c)")
                sp.dma_start(dst, out[:, half]).then_inc(stored[half], 16)
                if half == 1 and b + 2 < IMG:
                    load(b + 2)
            for half in range(2):
                sp.wait_ge(stored[half], 16 * IMG)

        @block.tensor
        def _(pe):
            for n in range(2 * IMG):
                b, half = n // 2, n % 2
                if half == 0:
                    pe.wait_ge(loaded[b % 2], 16 * (b // 2 + 1))
                for t in range(T):
                    m = n * T + t
                    if m >= 8:
                        pe.wait_ge(copied_d if t % 2 else copied_a, (m - 8) // 2 + 1)
                    nc.tensor.matmul(bank[:, m % 8], w["dft"][:, half], rows[:, b % 2, NT * t:NT * (t + 1)],
                                     start=True, stop=True).then_inc(transformed, 1)

        @block.scalar
        def _(act):
            for n in range(2 * IMG):
                for t in range(0, T, 2):
                    m = n * T + t
                    act.wait_ge(transformed, m + 1)
                    if n >= 2:
                        act.wait_ge(stored[n % 2], 16 * (n // 2))
                    nc.scalar.activation(out[:, n % 2, NT * t:NT * (t + 1)], bank[:, m % 8],
                                         ACT.Copy).then_inc(copied_a, 1)

        @block.vector
        def _(dve):
            for n in range(2 * IMG):
                for t in range(1, T, 2):
                    m = n * T + t
                    dve.wait_ge(transformed, m + 1)
                    if n >= 2:
                        dve.wait_ge(stored[n % 2], 16 * (n // 2))
                    nc.vector.tensor_copy(out[:, n % 2, NT * t:NT * (t + 1)], bank[:, m % 8]).then_inc(copied_d, 1)


def matrices_stage(nc, tag, w, m_high, m_low):
    with ExitStack() as ctx:
        s = Scope(nc, ctx, tag)
        raw = s.sb("raw", [C, 2, 4, FILTERS, C])
        acc = s.sb("acc", [C, 2, FILTERS, C])
        loaded = s.sem("loaded")
        step = s.sem("step")
        block = ctx.enter_context(nc.Block())

        @block.sync
        def _(sp):
            for k, name in enumerate(("m_plus", "m_minus")):
                sp.dma_start(raw[:, k], w[name]).then_inc(loaded, 16)

        @block.vector
        def _(dve):
            count = 0

            def do(*instructions):
                nonlocal count
                for instruction in instructions:
                    instruction.then_inc(step, 1)
                count += len(instructions)
                dve.wait_ge(step, count)

            weight = w["weight"]
            dve.wait_ge(loaded, 32)
            do(*[nc.vector.tensor_scalar(acc[:, k], raw[:, k, 0], weight[:, 0:1], None, ALU.mult) for k in range(2)])
            for i in range(1, 4):
                do(*[nc.vector.scalar_tensor_tensor(out=acc[:, k], in0=raw[:, k, i], scalar=weight[:, i:i + 1],
                                                    in1=acc[:, k], op0=ALU.mult, op1=ALU.add) for k in range(2)])
            both = raw[:, 0, 0:2]
            do(nc.vector.tensor_tensor(both[:, 0], acc[:, 0], acc[:, 1], ALU.add),
               nc.vector.tensor_tensor(both[:, 1], acc[:, 0], acc[:, 1], ALU.subtract))
            sigma = w["sigma4"][:].unsqueeze(2).to_broadcast([C, FILTERS, C])
            do(*[nc.vector.tensor_tensor(acc[:, k], both[:, k], sigma, ALU.mult) for k in range(2)])
            high = m_high[:].rearrange("d (k l) e -> d l k e", l=2)
            low = m_low[:].rearrange("d (k l) e -> d l k e", l=2)
            do(*[nc.vector.tensor_copy(high[:, k], acc[:, k]) for k in range(2)])
            do(*[nc.vector.tensor_tensor(low[:, k], acc[:, k], high[:, k].bitcast(F32), ALU.subtract)
                 for k in range(2)])


def spectral_stage(nc, tag, m_high, m_low, gen_high, gen_low, uhat_dram, yhat_dram):
    with ExitStack() as ctx:
        s = Scope(nc, ctx, tag)
        raw = s.sb("raw", [C, 2, IMG, 2, C])
        u_high = s.sb("u_high", [C, 3, IMG, 2, C], F32R)
        u_low = s.sb("u_low", [C, 3, IMG, 2, C], F32R)
        Z = 129
        toeplitz = s.sb("toeplitz", [C, 2, 2, 2, Q4, Z], F32R)
        big_high = s.sb("big_high", [C, 2, 2, IMG, Q4, C], F32R)
        big_low = s.sb("big_low", [C, 2, 2, IMG, Q4, C], F32R)
        y_out = s.sb("y_out", [C, 2, 2, NT])
        u_bank = s.ps("u_bank", [C, 2, 2, NT])
        y_bank = s.ps("y_bank", [C, 2, 2, NT])
        raw_loaded = s.sem("raw_loaded")
        split = s.sem("split")
        toeplitz_loaded = [s.sem(f"toeplitz_loaded{k}") for k in range(2)]
        filled = s.sem("filled")
        high_ready = s.sem("high_ready")
        low_ready = s.sem("low_ready")
        projected = s.sem("projected")
        y_copied = s.sem("y_copied")
        y_stored = s.sem("y_stored")
        block = ctx.enter_context(nc.Block())

        FILLS = 8 * GROUPS
        HALVES = 2 * GROUPS

        def frequencies(eng, do):
            do(0, True)
            with eng.Fori(1, PLANES // 2) as f:
                do(f, False)

        @block.sync
        def _(sp):
            def load_u(f):
                for part in range(2):
                    for b in range(IMG):
                        src = uhat_dram[bass.ds(2 * f + part, 1), :, b].rearrange(
                            "o x (s p) c -> (o x) s (p c)", p=2)
                        sp.dma_start(raw[:, part, b].rearrange("s p c -> s (p c)"),
                                     src).then_inc(raw_loaded, 16)

            def load_t(f, g):
                sp.wait_ge(filled, 64 * f + 8 * g + 8)
                for k, gen in enumerate((gen_high, gen_low)):
                    for part in range(2):
                        src = bass.AP(gen.tensor, (2 * f + part) * (QS * GENERATOR) + Q4 * g * GENERATOR,
                                      [[1, C], [GENERATOR, Q4], [1, Z]])
                        sp.dma_start(toeplitz[:, g % 2, k, part].bitcast(F32), src).then_inc(toeplitz_loaded[g % 2], 16)

            def store_y(f):
                sp.wait_ge(y_copied, f + 2)
                dst = yhat_dram[bass.ds(2 * f, 2)].rearrange("r e n -> e r n")
                sp.dma_start(dst, y_out[:].rearrange("e r p n -> e r (p n)")).then_inc(y_stored, 16)

            def each(f, first):
                for g in range(GROUPS):
                    load_t(f, g)
                    if g == 2 and not first:
                        store_y(f - 1)
                    if g == 3:
                        sp.wait_ge(split, 4 * f + 4)
                        load_u(f + 1)

            load_u(0)
            each(0, True)
            with sp.Fori(1, PLANES // 2 - 1) as f:
                each(f, False)
            f = PLANES // 2 - 1
            for g in range(GROUPS):
                load_t(f, g)
                if g == 2:
                    store_y(f - 1)
            store_y(f)
            sp.wait_ge(y_stored, 16 * (PLANES // 2 + 1))

        @block.tensor
        def _(pe):
            def moving(slot, k, part, pi):
                t = toeplitz[:, slot, k, part]
                if pi == 0:
                    return t[:, :, 0:C]
                ap = t.ap
                return bass.AP(t.tensor, t.offset, [list(ap[0]), [2 * Z, 2], [Z + 1, 2], [1, C]])

            def fill(f, g, pi, b, first):
                n = 64 * f + 8 * g + 4 * pi + b
                pe.wait_ge(low_ready, n + 1)
                for out_part in range(2):
                    if first:
                        terms = [(out_part, out_part)]
                    else:
                        terms = [(0, 0), (2, 1)] if out_part == 0 else [(1, 0), (0, 1)]
                    ops = [(u_x, k, kind, part) for kind, part in terms
                           for u_x, k in ((u_low, 0), (u_high, 1), (u_high, 0))]
                    for m, (u_x, k, kind, part) in enumerate(ops):
                        mm = nc.tensor.matmul(u_bank[:, b % 2, out_part], u_x[:, kind, b, pi],
                                              moving(g % 2, k, part, pi), start=(m == 0), stop=(m == len(ops) - 1))
                mm.then_inc(filled, 1)
                return mm

            def project(f, g, pi):
                m = 16 * f + 2 * g + pi
                pe.wait_ge(low_ready, 4 * m + 6)
                if g == 0 and pi == 0:
                    pe.wait_ge(y_copied, f + 1)
                for q in range(Q4):
                    po = pi ^ (q % 2)
                    for part in range(2):
                        for k, (m_x, big) in enumerate(((m_low, big_high), (m_high, big_low), (m_high, big_high))):
                            mm = nc.tensor.matmul(y_bank[:, part, po], m_x[:, Q4 * g + q], big[:, pi, part, :, q],
                                                  start=(g == 0 and pi == 0 and q < 2 and k == 0),
                                                  stop=(g == GROUPS - 1 and pi == 1 and q >= 2 and k == 2),
                                                  skip_group_check=True)
                mm.then_inc(projected, 1)

            def each(f, first):
                pe.wait_ge(split, 4 * f + 4)
                for g in range(GROUPS):
                    pe.wait_ge(toeplitz_loaded[g % 2], (4 * f + g // 2 + 1) * 64)
                    for pi in range(2):
                        for b in range(IMG):
                            fill(f, g, pi, b, first)
                            if b == 1 and (g or pi):
                                project(f, g if pi else g - 1, 1 - pi)
                project(f, GROUPS - 1, 1)

            frequencies(pe, each)

        @block.scalar
        def _(act):
            def each(f, first):
                for g in range(GROUPS):
                    for pi in range(2):
                        act.wait_ge(projected, HALVES * f + 2 * g + pi + 1)
                        for b in range(IMG):
                            act.wait_ge(filled, FILLS * f + 8 * g + 4 * pi + b + 17)
                            nc.scalar.activation(big_high[:, pi, :, b], u_bank[:, b % 2].rearrange(
                                "c r (q t) -> c r q t", q=Q4), ACT.Copy).then_inc(high_ready, 1)
                act.wait_ge(projected, HALVES * (f + 1) + 2)
                act.wait_ge(y_stored, 16 * f + 16)
                nc.scalar.activation(y_out[:], y_bank[:], ACT.Copy).then_inc(y_copied, 1)

            frequencies(act, each)

        @block.vector
        def _(dve):
            def each(f, first):
                dve.wait_ge(raw_loaded, 128 * f + 128)
                dve.wait_ge(filled, FILLS * f + 16)
                nc.vector.tensor_copy(u_high[:, 0:2], raw[:]).then_inc(split, 1)
                dve.wait_ge(split, 4 * f + 1)
                nc.vector.tensor_tensor(u_low[:, 0:2], raw[:], u_high[:, 0:2].bitcast(F32),
                                        ALU.subtract).then_inc(split, 1)
                nc.vector.tensor_scalar(u_high[:, 2], u_high[:, 1].bitcast(F32), -1.0, None,
                                        ALU.mult).then_inc(split, 1)
                dve.wait_ge(split, 4 * f + 2)
                nc.vector.tensor_scalar(u_low[:, 2], u_low[:, 1].bitcast(F32), -1.0, None,
                                        ALU.mult).then_inc(split, 1)
                for g in range(GROUPS):
                    for pi in range(2):
                        for b in range(IMG):
                            dve.wait_ge(high_ready, FILLS * f + 8 * g + 4 * pi + b + 1)
                            nc.vector.tensor_tensor(big_low[:, pi, :, b], u_bank[:, b % 2].rearrange(
                                "c r (q t) -> c r q t", q=Q4), big_high[:, pi, :, b].bitcast(F32),
                                ALU.subtract).then_inc(low_ready, 1)

            dve.sem_inc(filled, 16)
            dve.sem_inc(low_ready, 2)
            dve.sem_inc(projected, 2)
            dve.sem_inc(y_copied, 1)
            dve.sem_inc(y_stored, 16)
            frequencies(dve, each)


def inverse_stage(nc, tag, w, yhat_dram, x_dram, out_dram):
    CH = 4
    CHUNKS = 32 // CH
    OUT = 4 * BLOCKS
    with ExitStack() as ctx:
        s = Scope(nc, ctx, tag)
        rows = s.sb("rows", [C, 2, CH, 2, NT])
        x = s.sb("x", [OUT, 2, CH, IMG, 2 * 128])
        bank = s.ps("bank", [C, 8, NT])
        rows_loaded = [s.sem(f"rows_loaded{k}") for k in range(2)]
        x_loaded = [s.sem(f"x_loaded{k}") for k in range(2)]
        transformed = s.sem("transformed")
        added = s.sem("added")
        stored = [s.sem(f"stored{k}") for k in range(2)]
        block = ctx.enter_context(nc.Block())
        N = 2 * CH

        def by_block(dram, chunk, xx):
            rows_of = dram[32 * xx + CH * chunk:32 * xx + CH * (chunk + 1), :]
            return rows_of.rearrange("c (b j t) -> j (c b) t", b=IMG, j=BLOCKS)

        @block.sync
        def _(sp):
            def load(c):
                if c >= 2:
                    sp.wait_ge(transformed, N * (c - 1))
                src = yhat_dram.rearrange("p (x e) n -> (p x) e n", x=4)[:, CH * c:CH * (c + 1)]
                sp.dma_start(rows[:, c % 2].rearrange("p e r n -> p e (r n)"), src).then_inc(rows_loaded[c % 2], 16)
                if c >= 2:
                    sp.wait_ge(stored[c % 2], 64 * (c // 2))
                for xx in range(4):
                    sp.dma_start(x[BLOCKS * xx:BLOCKS * (xx + 1), c % 2].rearrange("j c b t -> j (c b) t"),
                                 by_block(x_dram, c, xx)).then_inc(x_loaded[c % 2], 16)

            load(0)
            load(1)
            for c in range(CHUNKS):
                sp.wait_ge(added, N * (c + 1))
                for xx in range(4):
                    sp.dma_start(by_block(out_dram, c, xx),
                                 x[BLOCKS * xx:BLOCKS * (xx + 1), c % 2].rearrange("j c b t -> j (c b) t")
                                 ).then_inc(stored[c % 2], 16)
                if c + 2 < CHUNKS:
                    load(c + 2)
            for slot in range(2):
                sp.wait_ge(stored[slot], 64 * CHUNKS // 2)

        @block.tensor
        def _(pe):
            for c in range(CHUNKS):
                pe.wait_ge(rows_loaded[c % 2], 16 * (c // 2 + 1))
                for k in range(N):
                    if c:
                        pe.wait_ge(added, N * (c - 1) + k + 1)
                    nc.tensor.matmul(bank[0:OUT, k], w["inverse"][:], rows[:, c % 2, k // 2, k % 2],
                                     start=True, stop=True).then_inc(transformed, 1)

        @block.vector
        def _(dve):
            for c in range(CHUNKS):
                dve.wait_ge(x_loaded[c % 2], 64 * (c // 2 + 1))
                for k in range(N):
                    dve.wait_ge(transformed, N * c + k + 1)
                    tile = x[:, c % 2, k // 2].rearrange("p b (t r) -> p b t r", r=2)[:, :, ::-1, k % 2]
                    nc.vector.scalar_tensor_tensor(out=tile, in0=bank[0:OUT, k].rearrange("p (b t) -> p b t", b=IMG),
                                                   scalar=w["mask_col"][:, 0:1], in1=tile, op0=ALU.mult,
                                                   op1=ALU.add).then_inc(added, 1)


def metaformer(nc, a, out):
    with ExitStack() as ctx:
        def scratch(name, shape, dt=F32):
            return nc.dram_tensor(name, shape, dt).ap()

        turned_dram = scratch("turned", [TOK, C])
        x_dram = scratch("x_kept", [C, TOK])
        uhat_dram = scratch("uhat", [PLANES, 8, IMG, 32, C])
        yhat_dram = scratch("yhat", [PLANES, C, 2 * NT])
        gen_high = scratch("gen_high", [PLANES, QS, GENERATOR])
        gen_low = scratch("gen_low", [PLANES, QS, GENERATOR])

        def buffers(stack, names, tag="sb"):
            return {n: stack.enter_context(nc.sbuf_tensor(f"{tag}_{n}", list(a[n].shape), a[n].dtype)) for n in names}

        consts = buffers(ctx, ["ident", "mean"])
        load_stage(nc, "load_consts", [(consts[n][:], a[n]) for n in consts])
        small = {n: ctx.enter_context(nc.sbuf_tensor(f"sb_{n}", shape, F32)) for n, shape in (
            ("weight", [C, 4]), ("segment", [C, 4]), ("sigma4", [C, FILTERS]), ("mask_col", [64, 1]))}
        with ExitStack() as held:
            wide = held.enter_context(nc.sbuf_tensor("wide", [C, PAD + TOK + PAD], F32))
            xh = wide[:, PAD:PAD + TOK]
            load_stage(nc, "load_x", [(xh, a["x"])])
            layernorm_stage(nc, "norm_c0", consts, xh, xh, 1e-6)
            layernorm_stage(nc, "norm_m0", consts, xh, xh, 1e-5)
            with ExitStack() as inner:
                names = ["order", "in", "x_proj", "dt_proj", "out_proj", "select", "less", "mask", "columns", "a_log",
                         "conv_w"]
                w = buffers(inner, names)
                load_stage(nc, "load_mamba", [(w[n][:], a[n]) for n in names])
                w["x"], w["dt"], w["out"] = w["x_proj"], w["dt_proj"], w["out_proj"]
                for n, first, count in COLUMNS:
                    w[n] = w["columns"][:, first:first + count]
                mamba_stage(nc, "mamba", consts, w, wide)
            with ExitStack() as inner:
                x = inner.enter_context(nc.sbuf_tensor("x_sb", [C, TOK], F32))
                w = buffers(inner, ["gamma", "beta", "w_p", "b_p"], tag="proj")
                load_stage(nc, "load_proj", [(x[:], a["x"])] + [(w[n][:], a[n]) for n in w])
                layernorm_stage(nc, "norm_m1", consts, xh, xh, 1e-5, gamma=w["gamma"][:, 0:1])
                project_stage(nc, "project", w, xh, x)
                layernorm_stage(nc, "norm_t0", consts, x, xh, 1e-5)
                with ExitStack() as moe:
                    names = ["router", "expert", "bias", "router_b", "index"]
                    w = buffers(moe, names)
                    load_stage(nc, "load_experts", [(w[n][:], a[n]) for n in names])
                    experts_stage(nc, "experts", consts, w, wide[:, PAD:], x)
                layernorm_stage(nc, "norm_c1", consts, x, xh, 1e-6)
                with ExitStack() as sweep:
                    w = buffers(sweep, ["sweep", "sweep_b"])
                    load_stage(nc, "load_sweep", [(w[n][:], a[n]) for n in w])
                    sweep_stage(nc, "sweep", w, xh)
                add_stage(nc, "add", x[:], xh)
                layernorm_stage(nc, "norm_t1", consts, x, xh, 1e-5)
                with ExitStack() as ar:
                    names = ["log_weights", "gumbel", "sigma", "segment_of", "m_u_all"]
                    w = buffers(ar, names)
                    w.update(small)
                    w["block_mask"] = ar.enter_context(nc.sbuf_tensor("sb_block_mask", [64, 4], F32))
                    w["m_u"] = ar.enter_context(nc.sbuf_tensor("sb_m_u", [C, 3, C], F32))
                    load_stage(nc, "load_ar", [(w[n][:], a[n]) for n in names])
                    choice_stage(nc, "choice", w)
                    autoregressive_stage(nc, "ar", w, xh, x)
                turn_stage(nc, "turn", consts, xh, x[:], turned_dram, x_dram)
        with ExitStack() as inner:
            w = buffers(inner, ["dft", "dft_taps"])
            w["phi"] = a["phi"]
            load_stage(nc, "load_dft", [(w[n][:], a[n]) for n in ("dft", "dft_taps")])
            with ExitStack() as g:
                generator_stage(nc, "generator", w, gen_high, gen_low)
            forward_stage(nc, "forward", w, turned_dram, uhat_dram)
        with ExitStack() as inner:
            m_high = inner.enter_context(nc.sbuf_tensor("m_high", [C, QS, C], F32R))
            m_low = inner.enter_context(nc.sbuf_tensor("m_low", [C, QS, C], F32R))
            matrices_stage(nc, "matrices", dict(small, m_plus=a["m_plus"], m_minus=a["m_minus"]), m_high, m_low)
            spectral_stage(nc, "spectral", m_high, m_low, gen_high, gen_low, uhat_dram, yhat_dram)
        with ExitStack() as inner:
            w = buffers(inner, ["inverse"])
            load_stage(nc, "load_inverse", [(w["inverse"][:], a["inverse"])])
            inverse_stage(nc, "inverse", dict(small, inverse=w["inverse"]), yhat_dram, x_dram, out)


def kernel(**inputs):
    import math

    import numpy as np
    from concourse import bacc
    from concourse.bass_utils import run_bass_kernel_spmd

    import ml_dtypes

    i = {k: np.asarray(v) for k, v in inputs.items()}
    m = {k[len("L0_conv_"):]: v for k, v in i.items() if k.startswith("L0_conv_")}
    h = INNER // 2

    def over_partitions(v, rows=C):
        return np.ascontiguousarray(np.broadcast_to(v[None], (rows, *v.shape)))

    def by_half(v):
        return np.ascontiguousarray(v.reshape(2, h, *v.shape[1:]).swapaxes(0, 1))

    order = np.zeros((C, 2, C), np.float32)
    for c in range(C):
        order[c, 0, c] = 1
        order[(c % 8) * 16 + c // 8, 1, c] = 1
    select = np.zeros((96, 2 * STATES, C), ml_dtypes.bfloat16)
    for k in range(96):
        select[k, k % 32] = 1
    less = np.zeros((96, 2), np.float32)
    less[32:, 0] = -1
    less[64:, 1] = -1
    mask = np.ones((C, PAIRS + 1), np.float32)
    mask[:, ::PAIRS // IMG] = 0

    def plane(p, j, back):
        f, part = (16 * p, 0) if p < 2 else (p // 2, p % 2)
        angle = 2 * math.pi * f * j / PLANES
        value = math.cos(angle) if part == 0 else -math.sin(angle)
        return value * ((1 if p < 2 else 2) / PLANES if back else 1)

    dft = np.zeros((BLOCKS, 8, 2, 16, 8), np.float32)
    for j in range(BLOCKS):
        for p in range(PLANES):
            for x in range(8):
                dft[j, x, p // 16, p % 16, x] = plane(p, j, False)
    inverse = np.zeros((PLANES, 4, 4, BLOCKS), np.float32)
    for p in range(PLANES):
        for j in range(BLOCKS):
            for x in range(4):
                inverse[p, x, x, j] = plane(p, j, True)
    dft_taps = np.array([[[plane(p, j + v, False) for p in range(PLANES)] for v in range(2)]
                         for j in range(BLOCKS)], np.float32)
    segment_of = np.zeros((64, 4), np.float32)
    for r in range(64):
        segment_of[r, sum(r % BLOCKS >= edge for edge in (2, 4, 8))] = 1

    x_dbl = np.zeros((C, INNER), np.float32)
    rank = m["W_dt"].shape[1]
    for part in range(3):
        x_dbl[32 * part:32 * (part + 1)] = m["W_x"][rank:]
    x_dbl[96:96 + rank] = m["W_x"][:rank]
    dt_proj = np.zeros((C, INNER), np.float32)
    dt_proj[96:96 + rank] = m["W_dt"].T
    directions = "durl"
    phi = i["L1_ffn_phi"].reshape(BLOCKS, 128, 2, FILTERS)[:, ::-1]
    arrays = {
        "x": i["x"].reshape(IMG, C, LEN).transpose(1, 0, 2).reshape(C, TOK),
        "ident": np.eye(C, dtype=np.float32), "mean": np.full((C, C), 1 / C, np.float32),
        "order": order, "select": select, "less": less, "mask": mask,
        "in": m["W_in"].T, "x_proj": by_half(x_dbl.T), "dt_proj": dt_proj, "out_proj": by_half(m["W_out"].T),
        "gamma": m["gamma"][:, None], "beta": m["beta"][:, None],
        "columns": np.concatenate([
            m["gamma"][:, None], m["beta"][:, None], by_half(m["conv_b"]), by_half(m["b_dt"]), by_half(m["D_skip"]),
            over_partitions(np.concatenate([m["s1"], m["s2"]]))], 1),
        "a_log": by_half(m["A_log"]), "conv_w": over_partitions(m["conv_w"][:, 0].T),
        "w_p": m["W_p"].T, "b_p": m["b_p"][:, None],
        "router": i["L0_ffn_router_w"], "expert": i["L0_ffn_expert_w"].transpose(1, 0, 2),
        "bias": i["L0_ffn_expert_b"],
        "router_b": over_partitions(np.broadcast_to(i["L0_ffn_router_b"], (SUB, EXPERTS))),
        "index": over_partitions(np.arange(EXPERTS, dtype=np.float32)),
        "sweep": np.stack([i["L1_conv_w_" + d] for d in directions]).transpose(2, 0, 3, 1),
        "sweep_b": np.stack([i["L1_conv_b_" + d] for d in directions], 1),
        "log_weights": over_partitions(i["L1_ffn_log_weights"]), "gumbel": over_partitions(i["L1_ffn_gumbel"]),
        "sigma": over_partitions(i["L1_ffn_sigma"]), "segment_of": segment_of,
        "m_u_all": i["L1_ffn_M_u"].transpose(2, 0, 1, 3),
        "m_plus": i["L1_ffn_M_phi_plus"].transpose(2, 0, 1, 3),
        "m_minus": i["L1_ffn_M_phi_minus"].transpose(2, 0, 1, 3),
        "phi": phi.transpose(0, 3, 2, 1).reshape(BLOCKS, QS, 128),
        "dft": dft.reshape(C, 2, C), "inverse": inverse.reshape(C, 64), "dft_taps": dft_taps,
    }
    nc = bacc.Bacc("TRN2", target_bir_lowering=False, num_devices=1)
    arrays = {f"in_{k}": np.ascontiguousarray(v) for k, v in arrays.items()}
    args = {k[3:]: nc.dram_tensor(k, v.shape, mybir.dt.from_np(v.dtype), kind="ExternalInput").ap()
            for k, v in arrays.items()}
    out = nc.dram_tensor("out", (C, TOK), F32, kind="ExternalOutput").ap()
    metaformer(nc, args, out)
    result = run_bass_kernel_spmd(nc, [arrays], core_ids=[0]).results[0]["out"]
    return np.ascontiguousarray(result.reshape(C, IMG, LEN).transpose(1, 0, 2)).reshape(IMG, C, SIDE, SIDE)
```

```python
from contextlib import ExitStack

import concourse.bass as bass
from concourse import mybir

F32 = mybir.dt.float32
F32R = mybir.dt.float32r
BF16 = mybir.dt.bfloat16
U32 = mybir.dt.uint32
ALU = mybir.AluOpType
ACT = mybir.ActivationFunctionType
AX = mybir.AxisListType

C = 128
IMG = 4
LEN = 4096
TOK = IMG * LEN
SIDE = 64
NT = 512
QUAD = 4 * NT


class Scope:

    semaphores = []

    def __init__(self, nc, ctx, tag):
        self.nc, self.ctx, self.tag = nc, ctx, tag

    def sb(self, name, shape, dt=F32):
        return self.ctx.enter_context(self.nc.sbuf_tensor(f"{self.tag}_{name}", shape, dt))

    def ps(self, name, shape, dt=F32):
        return self.ctx.enter_context(self.nc.psum_tensor(f"{self.tag}_{name}", shape, dt))

    def sem(self, name):
        self.semaphores.append(self.nc.alloc_semaphore(f"{self.tag}_{name}"))
        return self.semaphores[-1]

    @classmethod
    def recycle(cls, nc):
        nc.clear_and_free_semaphores(cls.semaphores)
        cls.semaphores = []
        nc.all_engine_barrier()


def load_stage(nc, tag, pairs):
    with ExitStack() as ctx:
        s = Scope(nc, ctx, tag)
        moved = s.sem("moved")
        block = ctx.enter_context(nc.Block())

        @block.sync
        def _(sp):
            for dst, src in pairs:
                sp.dma_start(dst, src).then_inc(moved, 16)
            sp.wait_ge(moved, 16 * len(pairs))


def layernorm_stage(nc, tag, consts, src, dst, eps, gamma=None):
    ROUNDS = TOK // (2 * NT)
    STEPS = ROUNDS + 2
    LOOPS = (ROUNDS - 2) // 3
    with ExitStack() as ctx:
        s = Scope(nc, ctx, tag)
        square = s.sb("square", [C, 3, 2, NT])
        deviation = s.sb("deviation", [C, 3, 8])
        rstd = s.sb("rstd", [C, 3, 8])
        eps_col = s.sb("eps", [C, 1])
        bank = s.ps("bank", [C, 3, 2, NT])
        var_bank = s.ps("var", [C, 2, NT])
        mean_ready = s.sem("mean_ready")
        eps_set = s.sem("eps_set")
        centred = s.sem("centred")
        squared = s.sem("squared")
        var_ready = s.sem("var_ready")
        std_ready = s.sem("std_ready")
        rstd_ready = s.sem("rstd_ready")
        spread = s.sem("spread")
        normed = s.sem("normed")
        block = ctx.enter_context(nc.Block())

        def cols(r, t):
            return bass.ds(r * (2 * NT) + t * NT, NT)

        def pipeline(eng, do):
            for r in range(2):
                do(r, r % 3, r % 2, True, r >= 1, False)
            with eng.Fori(0, LOOPS // 2) as i:
                for k in range(6):
                    do(6 * i + (2 + k), (2 + k) % 3, k % 2, True, True, True)
            for r in range(2 + 6 * (LOOPS // 2), STEPS):
                do(r, r % 3, r % 2, r < ROUNDS, r <= ROUNDS, True)

        @block.tensor
        def _(pe):
            def step(r, slot, parity, mean, var, norm):
                if mean:
                    for t in range(2):
                        pe.wait_ge(normed, 2 * r + t + 1)
                        nc.tensor.matmul(bank[:, slot, t], consts["mean"][:], src[:, cols(r, t)],
                                         start=True, stop=True).then_inc(mean_ready, 1)
                if norm:
                    pe.wait_ge(rstd_ready, r - 1)
                    for t in range(2):
                        for k in range(4):
                            at = 4 * t + k
                            mm = nc.tensor.matmul(bank[:, (slot + 1) % 3, t, 128 * k:128 * k + 128],
                                                  rstd[:, (slot + 1) % 3, at:at + 1].to_broadcast([C, C]),
                                                  consts["ident"][:], start=True, stop=True)
                        mm.then_inc(spread, 1)
                if var:
                    pe.wait_ge(std_ready, r)
                    for t in range(2):
                        pe.wait_ge(squared, 2 * r + t - 1)
                        for k in range(4):
                            at = 4 * t + k
                            mm = nc.tensor.matmul(var_bank[:, 1 - parity, at:at + 1],
                                                  square[:, (slot + 2) % 3, t, 128 * k:128 * k + 128],
                                                  consts["mean"][:, 0:1], start=True, stop=True)
                    mm.then_inc(var_ready, 1)

            pipeline(pe, step)

        @block.scalar
        def _(act):
            act.wait_ge(eps_set, 1)

            def step(r, slot, parity, mean, var, norm):
                if mean:
                    for t in range(2):
                        act.wait_ge(centred, 2 * r + t + 1)
                        nc.scalar.activation(square[:, slot, t], dst[:, cols(r, t)], ACT.Square).then_inc(squared, 1)
                if var:
                    act.wait_ge(var_ready, r)
                    nc.scalar.activation(deviation[:, (slot + 2) % 3], var_bank[:, 1 - parity, 0:8], ACT.Sqrt,
                                         bias=eps_col[:, 0:1]).then_inc(std_ready, 1)

            pipeline(act, step)

        @block.vector
        def _(dve):
            def step(r, slot, parity, mean, var, norm):
                if mean:
                    for t in range(2):
                        dve.wait_ge(mean_ready, 2 * r + t + 1)
                        nc.vector.tensor_tensor(dst[:, cols(r, t)], src[:, cols(r, t)], bank[:, slot, t],
                                                ALU.subtract).then_inc(centred, 1)
                if norm:
                    for t in range(2):
                        dve.wait_ge(spread, 2 * r + t - 3)
                        tile = dst[:, cols(r - 2, t)]
                        if gamma is None:
                            nc.vector.tensor_tensor(tile, tile, bank[:, (slot + 1) % 3, t], ALU.mult).then_inc(normed, 1)
                        else:
                            nc.vector.scalar_tensor_tensor(out=tile, in0=tile, scalar=gamma,
                                                           in1=bank[:, (slot + 1) % 3, t], op0=ALU.mult,
                                                           op1=ALU.mult).then_inc(normed, 1)
                if var:
                    dve.wait_ge(std_ready, r + 2)
                    nc.vector.reciprocal(rstd[:, (slot + 2) % 3], deviation[:, (slot + 2) % 3]).then_inc(rstd_ready, 1)

            nc.vector.memset(eps_col[:], eps).then_inc(eps_set, 1)
            dve.sem_inc(normed, 6)
            dve.sem_inc(std_ready, 2)
            pipeline(dve, step)


INNER = 2 * C
STATES = 16
TAPS = 4
HIST = TAPS - 1
PE_AT = dict(order=1, conv=(4, 6), z=8, x=9, dt=10, out=13)
ACT_AT = dict(order=5, silu=10, x=11, dt=12)
DVE_AT = dict(history=1, rest=9, round=11, parts=12, skip=13)
POOL_AT = dict(middle=10, steps=12, store=15)
PAIRS = TOK // (2 * NT)
COLUMNS = (("gamma", 0, 1), ("beta", 1, 1), ("conv_b", 2, 2), ("b_dt", 4, 2), ("d", 6, 2), ("s", 8, 2))
PAD = NT


def mamba_stage(nc, tag, consts, w, xh):
    with ExitStack() as ctx:
        s = Scope(nc, ctx, tag)
        x_in = s.sb("x_in", [C, 2, 2, HIST + NT])
        u = s.sb("u", [C, 2, 2, NT])
        gate = s.sb("gate", [C, 2, 2, NT])
        dt = s.sb("dt", [C, 2, 2, NT])
        dtu = s.sb("dtu", [C, 2, 2, NT])
        x_dbl = s.sb("x_dbl", [C, NT])
        bc_high = s.sb("bc_high", [96, NT], BF16)
        bc_rest = s.sb("bc_rest", [96, NT])
        bc_mid = s.sb("bc_mid", [96, NT], BF16)
        bc = s.sb("bc", [96, 2, NT], BF16)
        soft_abs = s.sb("soft_abs", [C, 2, NT])
        soft_pos = s.sb("soft_pos", [C, 2, NT])
        soft_ln = s.sb("soft_ln", [C, 2, NT])
        decay = s.sb("decay", [C, 4, 2, NT])
        inject = s.sb("inject", [C, 2, 2, NT])
        h = s.sb("h", [C, 4, 2, NT])
        hc = s.sb("hc", [C, 2, 2, NT])
        carry = s.sb("carry", [C, 2, STATES, 2])
        y1 = s.sb("y1", [C, 2, NT])
        y2 = s.sb("y2", [C, 2, NT])
        skip = s.sb("skip", [C, 2, NT])
        zero = s.sb("zero", [C, 1])
        conv_in = w["conv_w"]
        neg_a = w["a_log"]
        front = s.ps("front", [C, 2, NT])
        b_bank = s.ps("b_bank", [C, 2, NT])
        c_bank = s.ps("c_bank", [C, 2, NT])
        y_bank = s.ps("y_bank", [C, 2, NT])

        fronted = s.sem("fronted")
        front_step = s.sem("front_step")
        hist_ready = s.sem("hist_ready")
        rounded = s.sem("rounded")
        dt_part = s.sem("dt_part")
        rest_ready = s.sem("rest_ready")
        mid_ready = s.sem("mid_ready")
        bc_ready = s.sem("bc_ready")
        dt_ready = s.sem("dt_ready")
        dtu_ready = s.sem("dtu_ready")
        b_ready = s.sem("b_ready")
        c_ready = s.sem("c_ready")
        summed = s.sem("summed")
        decayed = s.sem("decayed")
        injected = s.sem("injected")
        scanned = s.sem("scanned")
        carried = s.sem("carried")
        weighed = s.sem("weighed")
        y1_ready = s.sem("y1_ready")
        y2_ready = s.sem("y2_ready")
        out_ready = s.sem("out_ready")
        skip_ready = s.sem("skip_ready")
        stored = s.sem("stored")
        masked = s.sem("masked")
        zeroed = s.sem("zeroed")
        prepared = s.sem("prepared")
        a_ready = s.sem("a_ready")
        block = ctx.enter_context(nc.Block())

        def tile_cols(i, tile):
            return bass.ds(i * (2 * NT) + (PAD + tile * NT), NT)

        @block.tensor
        def _(pe):
            def front_order(i, U, q, first=False):
                if not first:
                    pe.wait_ge(front_step, 13 * U - 2)
                nc.tensor.matmul(front[:, 0], w["order"][:, q % 2], xh[:, tile_cols(i, q // 2)],
                                 start=True, stop=True).then_inc(fronted, 1)

            def front_conv(U, q, half, taps, first=False):
                if taps[0] == 0 and half == 0:
                    pe.wait_ge(front_step, 13 * U + 1)
                    pe.wait_ge(hist_ready, U + 1)
                if taps[0] == 0 and half == 1 and not first:
                    pe.wait_ge(skip_ready, U)
                for j in taps:
                    mm = nc.tensor.matmul(front[:, half], conv_in[:, j, half * C:(half + 1) * C],
                                          x_in[:, q % 2, q // 2, j:j + NT],
                                          start=(j == 0), stop=(j == TAPS - 1), skip_group_check=True)
                if taps[-1] == TAPS - 1:
                    mm.then_inc(fronted, 1)

            def front_z(U, q):
                for half in range(2):
                    pe.wait_ge(front_step, 13 * U + 2 + half)
                    nc.tensor.matmul(front[:, half], w["in"][:, INNER + half * C:INNER + (half + 1) * C],
                                     x_in[:, q % 2, q // 2, HIST:HIST + NT],
                                     start=True, stop=True).then_inc(fronted, 1)

            def front_x(U, q):
                pe.wait_ge(front_step, 13 * U + 4)
                nc.tensor.matmul(front[:, 0], w["x"][:, 0], u[:, q % 2, 0], start=True, stop=False)
                nc.tensor.matmul(front[:, 0], w["x"][:, 1], u[:, q % 2, 1], start=False,
                                 stop=True).then_inc(fronted, 1)

            def front_dt(U):
                pe.wait_ge(front_step, 13 * U + 6)
                nc.tensor.matmul(front[:, 1], w["dt"][:, 0:C], x_dbl[:], start=True, stop=True).then_inc(fronted, 1)
                pe.wait_ge(front_step, 13 * U + 7)
                nc.tensor.matmul(front[:, 0], w["dt"][:, C:INNER], x_dbl[:], start=True, stop=True).then_inc(fronted, 1)

            def out_proj(U, newest):
                pe.wait_ge(y2_ready, U + 2)
                pe.wait_ge(front_step, 13 * newest + 9)
                nc.tensor.matmul(front[:, 1], w["out"][:, 0], y2[:, 0], start=True, stop=False)
                nc.tensor.matmul(front[:, 1], w["out"][:, 1], y2[:, 1], start=False,
                                 stop=True).then_inc(out_ready, 1)

            def spread_b(g, n, slot):
                pe.wait_ge(injected, g + 1)
                nc.tensor.matmul(b_bank[:, n % 2], w["select"][:, n], bc[:, slot],
                                 start=True, stop=True).then_inc(b_ready, 1)

            def spread_c(g, n, slot):
                pe.wait_ge(weighed, g + 1)
                nc.tensor.matmul(c_bank[:, n % 2], w["select"][:, STATES + n], bc[:, slot],
                                 start=True, stop=True).then_inc(c_ready, 1)

            def add_up(n):
                for half in range(2):
                    mm = nc.tensor.matmul(y_bank[:, half], consts["ident"][:], hc[:, n % 2, half],
                                          start=(n == 0), stop=(n == STATES - 1), skip_group_check=True)
                mm.then_inc(summed, 1)

            pe.wait_ge(zeroed, 1)
            pe.wait_ge(prepared, 1)
            for half in range(2):
                nc.tensor.matmul(y_bank[:, half], consts["ident"][:], hc[:, 0, half], start=True, stop=False,
                                 skip_group_check=True)
            front_order(0, 0, 0, first=True)
            for half in range(2):
                front_conv(0, 0, half, range(TAPS), first=True)
            front_z(0, 0)
            front_x(0, 0)
            front_dt(0)
            with pe.Fori(0, PAIRS) as i:
                for q in range(4):
                    U = 4 * i + q
                    ni, nq = i + (q + 1) // 4, (q + 1) % 4
                    pe.wait_ge(bc_ready, U + 1)
                    for n in range(STATES):
                        g = 16 * U + n
                        if n != 4:
                            spread_b(g, n, q % 2)
                        spread_c(g, (n - 1) % STATES, (q if n else q - 1) % 2)
                        if n == 3:
                            spread_b(g + 1, n + 1, q % 2)
                            pe.wait_ge(y1_ready, U + 1)
                        add_up((n - 3) % STATES)
                        if n == PE_AT["order"]:
                            front_order(ni, U + 1, nq)
                        for half in range(2):
                            if n - PE_AT["conv"][half] in (0, 1):
                                first_tap = 2 * (n - PE_AT["conv"][half])
                                front_conv(U + 1, nq, half, range(first_tap, first_tap + 2))
                        if n == PE_AT["z"]:
                            front_z(U + 1, nq)
                        if n == PE_AT["x"]:
                            front_x(U + 1, nq)
                        if n == PE_AT["dt"]:
                            front_dt(U + 1)
                        if n == PE_AT["out"]:
                            out_proj(U, U + 1)
            U = 4 * PAIRS
            pe.wait_ge(bc_ready, U + 1)
            spread_b(16 * U, 0, 0)
            spread_c(16 * U, STATES - 1, 1)
            for k in range(3):
                pe.wait_ge(weighed, 16 * U + 1 + k)
                add_up(STATES - 3 + k)
            out_proj(U, U)

        @block.scalar
        def _(act):
            def act_order(U, q, first=False):
                act.wait_ge(fronted, 8 * U + 1)
                act.wait_ge(hist_ready, U + 1)
                nc.scalar.activation(x_in[:, q % 2, q // 2, HIST:HIST + NT], front[:, 0], ACT.Identity,
                                     bias=w["beta"][:, 0:1], scale=w["gamma"][:, 0:1]).then_inc(front_step, 1)

            def act_silu(U, q, first=False):
                slot = q % 2
                if not first:
                    act.wait_ge(y1_ready, U)
                    act.wait_ge(y2_ready, U + 1)
                for k in range(4):
                    act.wait_ge(fronted, 8 * U + 2 + k)
                    bias = w["conv_b"][:, k:k + 1] if k < 2 else 0.0
                    nc.scalar.activation((u, gate)[k // 2][:, slot, k % 2], front[:, k % 2], ACT.Silu,
                                         bias=bias).then_inc(front_step, 1)

            def act_x(U, first=False):
                act.wait_ge(fronted, 8 * U + 6)
                if not first:
                    act.wait_ge(bc_ready, U)
                nc.scalar.activation(x_dbl[:], front[:, 0], ACT.Copy).then_inc(front_step, 1)
                nc.scalar.activation(bc_high[:], front[0:96, 0], ACT.Copy).then_inc(front_step, 1)

            def act_dt(U, first=False):
                if not first:
                    act.wait_ge(dt_ready, U)
                for half in range(2):
                    act.wait_ge(fronted, 8 * U + 7 + half)
                    bias = w["b_dt"][:, half:half + 1]
                    nc.scalar.activation(soft_abs[:, half], front[:, 1 - half], ACT.Abs,
                                         bias=bias).then_inc(front_step, 1)
                    nc.scalar.activation(soft_pos[:, half], front[:, 1 - half], ACT.Relu,
                                         bias=bias).then_inc(front_step, 1)
                act.wait_ge(front_step, 13 * U + 11)
                nc.scalar.activation(soft_abs[:], soft_abs[:], ACT.Exp, scale=-1.0).then_inc(front_step, 1)
                act.wait_ge(front_step, 13 * U + 12)
                nc.scalar.activation(soft_ln[:], soft_abs[:], ACT.Ln, bias=1.0).then_inc(front_step, 1)

            nc.scalar.activation(neg_a[:], neg_a[:], ACT.Exp).then_inc(a_ready, 1)
            act.wait_ge(zeroed, 1)
            act_order(0, 0, first=True)
            act_silu(0, 0, first=True)
            act_x(0, first=True)
            act_dt(0, first=True)
            act.wait_ge(prepared, 1)
            with act.Fori(0, PAIRS) as i:
                for q in range(4):
                    U = 4 * i + q
                    act.wait_ge(dt_ready, U + 1)
                    for n in range(STATES):
                        g = 16 * U + n
                        act.wait_ge(scanned, g + 1)
                        for half in range(2):
                            e = nc.scalar.activation(decay[:, n % 4, half], dt[:, q % 2, half], ACT.Exp,
                                                     scale=neg_a[:, half, n:n + 1])
                        e.then_inc(decayed, 1)
                        if n == ACT_AT["order"]:
                            act_order(U + 1, (q + 1) % 4)
                        if n == ACT_AT["silu"]:
                            act_silu(U + 1, (q + 1) % 4)
                        if n == ACT_AT["x"]:
                            act_x(U + 1)
                        if n == ACT_AT["dt"]:
                            act_dt(U + 1)

        @block.vector
        def _(dve):
            def history(i, U, q, first=False):
                dst = x_in[:, q % 2, q // 2, 0:HIST]
                src = x_in[:, q % 2, 1 - q // 2, NT:NT + HIST]
                if first:
                    nc.vector.memset(dst, 0.0).then_inc(hist_ready, 1)
                    return
                dve.wait_ge(front_step, 13 * (U - 1) + 1)
                if q // 2:
                    nc.vector.tensor_copy(dst, src).then_inc(hist_ready, 1)
                else:
                    nc.vector.tensor_scalar(dst, src, w["mask"][:, bass.ds(i, 1)], None,
                                            ALU.mult).then_inc(hist_ready, 1)

            def round_trip(U, q):
                dve.wait_ge(front_step, 13 * U + 12)
                nc.vector.tensor_scalar(dt[:, q % 2], soft_abs[:], 1.0, 1.0, ALU.add,
                                        ALU.subtract).then_inc(rounded, 1)

            def rest(U):
                dve.wait_ge(front_step, 13 * U + 7)
                nc.vector.scalar_tensor_tensor(out=bc_rest[:], in0=bc_high[:], scalar=w["less"][:, 0:1],
                                               in1=x_dbl[0:96, :], op0=ALU.mult, op1=ALU.add).then_inc(rest_ready, 1)

            def parts(U, q, first=False):
                dve.wait_ge(mid_ready, U + 1)
                if not first:
                    dve.wait_ge(c_ready, 16 * U - 15)
                nc.vector.scalar_tensor_tensor(out=bc[:, q % 2], in0=bc_mid[:], scalar=w["less"][:, 1:2],
                                               in1=bc_rest[:], op0=ALU.mult, op1=ALU.add).then_inc(bc_ready, 1)

            def do_inject(g, n, slot):
                dve.wait_ge(b_ready, g + 1)
                dve.wait_ge(scanned, g + 3)
                nc.vector.tensor_tensor(inject[:, n % 2], dtu[:, slot],
                                        b_bank[:, n % 2].unsqueeze(1).to_broadcast([C, 2, NT]),
                                        ALU.mult).then_inc(injected, 1)

            def do_scan(g, n, v):
                dve.wait_ge(decayed, g + 1)
                dve.wait_ge(injected, g + 3)
                dve.wait_ge(carried, g + 1)
                dve.wait_ge(weighed, g + 1)
                for half in range(2):
                    sc = nc.vector.tensor_tensor_scan(h[:, n % 4, half], decay[:, n % 4, half],
                                                      inject[:, n % 2, half], carry[:, v, n, half:half + 1],
                                                      ALU.mult, ALU.add)
                sc.then_inc(scanned, 1)

            def do_weigh(g, n):
                dve.wait_ge(c_ready, g + 1)
                dve.wait_ge(summed, g + 1)
                dve.wait_ge(scanned, g + 4)
                nc.vector.tensor_tensor(hc[:, n % 2], h[:, n % 4],
                                        c_bank[:, n % 2].unsqueeze(1).to_broadcast([C, 2, NT]),
                                        ALU.mult).then_inc(weighed, 1)

            def end_y(U, q):
                dve.wait_ge(summed, 16 * U + 3)
                dve.wait_ge(y2_ready, U + 1)
                for half in range(2):
                    y = nc.vector.scalar_tensor_tensor(out=y1[:, half], in0=u[:, (q - 1) % 2, half],
                                                       scalar=w["d"][:, half:half + 1], in1=y_bank[:, half],
                                                       op0=ALU.mult, op1=ALU.add)
                y.then_inc(y1_ready, 1)

            def end_skip(i, U, q):
                v, p = (q - 1) % 2, ((q - 1) // 2) % 2
                dve.wait_ge(out_ready, U + 2)
                if v == 0:
                    dve.wait_ge(stored, 2 * i + q // 2 + 1)
                nc.vector.scalar_tensor_tensor(out=skip[:, v], in0=x_in[:, v, p, HIST:HIST + NT],
                                               scalar=w["s"][:, v:v + 1], in1=front[:, 1],
                                               op0=ALU.mult, op1=ALU.add).then_inc(skip_ready, 1)

            for half in range(2):
                for j in range(TAPS):
                    cols = slice(half * C, (half + 1) * C)
                    nc.vector.tensor_tensor(conv_in[:, j, cols], conv_in[:, j, cols], w["in"][:, cols], ALU.mult)
            dve.wait_ge(a_ready, 1)
            nc.vector.tensor_scalar(neg_a[:], neg_a[:], -1.0, None, ALU.mult).then_inc(prepared, 1)
            for z in (x_in, hc, h, u, gate, carry, bc, zero):
                nc.vector.memset(z[:], 0.0)
            nc.vector.memset(xh[:, 0:PAD], 0.0)
            nc.vector.memset(xh[:, PAD + TOK:], 0.0).then_inc(zeroed, 1)
            dve.wait_ge(zeroed, 1)
            dve.sem_inc(injected, 2)
            dve.sem_inc(scanned, 4)
            dve.sem_inc(weighed, 2)
            dve.sem_inc(skip_ready, 1)
            history(0, 0, 0, first=True)
            rest(0)
            round_trip(0, 0)
            parts(0, 0, first=True)
            dve.wait_ge(dtu_ready, 1)
            do_inject(0, 0, 0)
            with dve.Fori(0, PAIRS) as i:
                for q in range(4):
                    U = 4 * i + q
                    ni, nq = i + (q + 1) // 4, (q + 1) % 4
                    if q < 2:
                        dve.wait_ge(carried, 16 * U + 1)
                        dve.wait_ge(scanned, 16 * U + 4)
                        nc.vector.tensor_scalar(carry[:, q % 2], carry[:, q % 2], w["mask"][:, bass.ds(i, 1)],
                                                None, ALU.mult).then_inc(masked, 1)
                        dve.wait_ge(masked, 2 * i + q + 1)
                    for n in range(STATES):
                        g = 16 * U + n
                        if n == 3:
                            end_y(U, q)
                        do_scan(g, n, q % 2)
                        if n == STATES - 1:
                            dve.wait_ge(dtu_ready, U + 2)
                        do_inject(g + 1, (n + 1) % STATES, (q if n < STATES - 1 else q + 1) % 2)
                        do_weigh(g, (n - 1) % STATES)
                        if n == DVE_AT["history"]:
                            history(ni, U + 1, nq)
                        if n == DVE_AT["skip"]:
                            end_skip(i, U, q)
                        if n == DVE_AT["rest"]:
                            rest(U + 1)
                        if n == DVE_AT["round"]:
                            round_trip(U + 1, nq)
                        if n == DVE_AT["parts"]:
                            parts(U + 1, nq)
            U = 4 * PAIRS
            do_weigh(16 * U, STATES - 1)
            end_y(U, 0)
            end_skip(PAIRS, U, 0)

        @block.gpsimd
        def _(pool):
            def middle(U):
                pool.wait_ge(rest_ready, U + 1)
                nc.gpsimd.tensor_tensor(bc_mid[:], bc_rest[:], zero[0:96].to_broadcast([96, NT]),
                                        ALU.add).then_inc(mid_ready, 1)

            def steps_dt(U, q, first=False):
                slot = dt[:, q % 2]
                pool.wait_ge(rounded, U + 1)
                nc.gpsimd.tensor_tensor(slot, soft_abs[:], slot, ALU.subtract).then_inc(dt_part, 1)
                pool.wait_ge(dt_part, 2 * U + 1)
                nc.gpsimd.tensor_tensor(slot, soft_pos[:], slot, ALU.add).then_inc(dt_part, 1)
                pool.wait_ge(front_step, 13 * U + 13)
                pool.wait_ge(dt_part, 2 * U + 2)
                nc.gpsimd.tensor_tensor(slot, soft_ln[:], slot, ALU.add).then_inc(dt_ready, 1)
                pool.wait_ge(dt_ready, U + 1)
                if not first:
                    pool.wait_ge(injected, 16 * U - 14)
                nc.gpsimd.tensor_tensor(dtu[:, q % 2], dt[:, q % 2], u[:, q % 2], ALU.mult).then_inc(dtu_ready, 1)

            def keep(g, n, v):
                pool.wait_ge(scanned, g + 5)
                last = h[:, n % 4, :, NT - 1]
                nc.gpsimd.tensor_tensor(carry[:, v, n], last, zero[:].to_broadcast([C, 2]),
                                        ALU.add).then_inc(carried, 1)

            def end_gate(U, q):
                pool.wait_ge(y1_ready, U + 1)
                pool.wait_ge(out_ready, U + 1)
                nc.gpsimd.tensor_tensor(y2[:], y1[:], gate[:, (q - 1) % 2], ALU.mult).then_inc(y2_ready, 1)

            def store(i, U, q):
                pool.wait_ge(skip_ready, U + 2)
                nc.gpsimd.tensor_tensor(xh[:, tile_cols(i, q // 2 - 1)], skip[:, 0], skip[:, 1],
                                        ALU.add).then_inc(stored, 1)

            pool.wait_ge(zeroed, 1)
            nc.gpsimd.memset(skip[:], 0.0)
            pool.sem_inc(carried, 2)
            pool.sem_inc(y2_ready, 1)
            pool.sem_inc(out_ready, 1)
            middle(0)
            steps_dt(0, 0, first=True)
            with pool.Fori(0, PAIRS) as i:
                for q in range(4):
                    U = 4 * i + q
                    for n in range(STATES):
                        keep(16 * U + n, n, q % 2)
                        if n == 3:
                            end_gate(U, q)
                        if n == POOL_AT["store"] and q % 2 == 0:
                            store(i, U, q)
                        if n == POOL_AT["middle"]:
                            middle(U + 1)
                        if n == POOL_AT["steps"]:
                            steps_dt(U + 1, (q + 1) % 4)
            U = 4 * PAIRS
            end_gate(U, 0)
            store(PAIRS, U, 0)


def project_stage(nc, tag, w, src, x):
    with ExitStack() as ctx:
        s = Scope(nc, ctx, tag)
        bank = s.ps("bank", [C, 4, NT])
        bias = s.sb("bias", [C, 1])
        projected = s.sem("projected")
        beta_ready = s.sem("beta_ready")
        bias_ready = s.sem("bias_ready")
        added = s.sem("added")
        block = ctx.enter_context(nc.Block())

        @block.tensor
        def _(pe):
            nc.tensor.matmul(bank[:, 0, 0:1], w["w_p"][:], w["beta"][:], start=True, stop=True).then_inc(beta_ready, 1)
            pe.wait_ge(bias_ready, 1)
            with pe.Fori(0, TOK // QUAD) as i:
                for t in range(4):
                    pe.wait_ge(added, 4 * i + t + 1)
                    nc.tensor.matmul(bank[:, t], w["w_p"][:], src[:, bass.ds(i * QUAD + t * NT, NT)],
                                     start=True, stop=True).then_inc(projected, 1)

        @block.vector
        def _(dve):
            dve.sem_inc(added, 4)
            dve.wait_ge(beta_ready, 1)
            nc.vector.tensor_tensor(bias[:], bank[:, 0, 0:1], w["b_p"][:], ALU.add).then_inc(bias_ready, 1)
            dve.wait_ge(bias_ready, 1)
            with dve.Fori(0, TOK // QUAD) as i:
                for t in range(4):
                    dve.wait_ge(projected, 4 * i + t + 1)
                    tile = x[:, bass.ds(i * QUAD + t * NT, NT)]
                    nc.vector.scalar_tensor_tensor(out=tile, in0=bank[:, t], scalar=bias[:, 0:1], in1=tile,
                                                   op0=ALU.add, op1=ALU.add).then_inc(added, 1)


EXPERTS = 8
SUB = NT // 128


def experts_stage(nc, tag, consts, w, xn, x):
    with ExitStack() as ctx:
        s = Scope(nc, ctx, tag)
        x_tile = s.sb("x_tile", [C, 2, NT])
        logits = s.sb("logits", [C, SUB, EXPERTS])
        best = s.sb("best", [C, SUB, 8])
        best_at = s.sb("best_at", [C, SUB, 8], U32)
        at = s.sb("at", [C, SUB, 2])
        gap = s.sb("gap", [C, SUB])
        ratio = s.sb("ratio", [C, SUB])
        denom = s.sb("denom", [C, SUB])
        share = s.sb("share", [C, SUB, 2])
        hot = s.sb("hot", [C, 2, SUB, EXPERTS])
        gates = s.sb("gates", [C, 2, SUB, EXPERTS])
        gates_t = s.sb("gates_t", [EXPERTS, NT])
        scaled = s.sb("scaled", [C, 2, EXPERTS, C])
        mixed = s.sb("mixed", [C, SUB, C])
        logit_bank = s.ps("logit_bank", [C, NT])
        expert_bank = s.ps("expert_bank", [C, 2, EXPERTS, C])
        gate_bank = s.ps("gate_bank", [C, NT])
        out_bank = s.ps("out_bank", [C, NT])
        copied = s.sem("copied")
        routed = s.sem("routed")
        step = s.sem("step")
        ratio_ready = s.sem("ratio_ready")
        turned = s.sem("turned")
        gates_ready = s.sem("gates_ready")
        expert_ready = s.sem("expert_ready")
        scaled_ready = s.sem("scaled_ready")
        mixed_ready = s.sem("mixed_ready")
        back = s.sem("back")
        added = s.sem("added")
        block = ctx.enter_context(nc.Block())
        TILES = TOK // NT
        ROUTER = 19

        @block.tensor
        def _(pe):
            def route(j, slot):
                pe.wait_ge(copied, j + 1)
                for k in range(SUB):
                    mm = nc.tensor.matmul(logit_bank[:, EXPERTS * k:EXPERTS * (k + 1)],
                                          x_tile[:, slot, 128 * k:128 * (k + 1)], w["router"][:],
                                          start=True, stop=True)
                mm.then_inc(routed, 1)

            def turn_back(j, slot, k):
                pe.wait_ge(mixed_ready, SUB * j + k + 1)
                nc.tensor.matmul(out_bank[:, 128 * k:128 * (k + 1)], mixed[:, k], consts["ident"][:],
                                 start=True, stop=False)
                nc.tensor.matmul(out_bank[:, 128 * k:128 * (k + 1)], w["bias"][:],
                                 gates_t[:, 128 * k:128 * (k + 1)], start=False, stop=True).then_inc(back, 1)

            def experts(j, slot, k):
                pe.wait_ge(scaled_ready, SUB * j + k + 1)
                for part in range(2):
                    mm = nc.tensor.matmul(expert_bank[:, k % 2, 4 * part:4 * (part + 1)],
                                          x_tile[:, slot, 128 * k:128 * (k + 1)],
                                          w["expert"][:, 4 * part:4 * (part + 1)], start=True, stop=True)
                mm.then_inc(expert_ready, 1)

            route(0, 0)
            experts(0, 0, 0)
            with pe.Fori(0, TILES // 2) as i:
                for slot in range(2):
                    j = 2 * i + slot
                    pe.wait_ge(step, ROUTER * (j + 1))
                    for k in range(SUB):
                        mm = nc.tensor.matmul(gate_bank[0:EXPERTS, 128 * k:128 * (k + 1)],
                                              gates[:, slot, k], consts["ident"][:], start=True, stop=True)
                    mm.then_inc(turned, 1)
                    experts(j, slot, 1)
                    route(j + 1, 1 - slot)
                    for k in range(SUB):
                        if k == 1:
                            pe.wait_ge(gates_ready, j + 1)
                            pe.wait_ge(added, j + 1)
                        if 0 < k < SUB - 1:
                            experts(j, slot, k + 1)
                        elif k:
                            experts(j + 1, 1 - slot, 0)
                        if k:
                            turn_back(j, slot, k - 1)
                    turn_back(j, slot, SUB - 1)

        @block.scalar
        def _(act):
            def copy(i, slot):
                nc.scalar.activation(x_tile[:, slot], xn[:, bass.ds(i * 2 * NT + slot * NT, NT)],
                                     ACT.Copy).then_inc(copied, 1)

            def ratios(j):
                act.wait_ge(step, ROUTER * j + 10)
                nc.scalar.activation(ratio[:], gap[:], ACT.Exp).then_inc(ratio_ready, 1)

            copy(0, 0)
            ratios(0)
            with act.Fori(0, TILES // 2) as i:
                for slot in range(2):
                    j = 2 * i + slot
                    act.wait_ge(turned, j + 1)
                    copy(i + slot, 1 - slot)
                    nc.scalar.activation(gates_t[:], gate_bank[0:EXPERTS, :], ACT.Copy).then_inc(gates_ready, 1)
                    ratios(j + 1)

        @block.vector
        def _(dve):
            def router(j, slot, part, first=False):
                done = ROUTER * j
                lanes = [C, SUB, EXPERTS]
                if part == 0:
                    dve.wait_ge(routed, j + 1)
                    nc.vector.tensor_tensor(logits[:].rearrange("p k e -> p (k e)"), logit_bank[:, 0:SUB * EXPERTS],
                                            w["router_b"][:].rearrange("p k e -> p (k e)"), ALU.add).then_inc(step, 1)
                if part == 1:
                    if first:
                        dve.wait_ge(step, done + 1)
                    for k in range(SUB):
                        nc.vector.max(out=best[:, k], in_=logits[:, k]).then_inc(step, 1)
                    dve.wait_ge(step, done + 5)
                    nc.vector.tensor_tensor(gap[:], best[:, :, 1], best[:, :, 0], ALU.subtract).then_inc(step, 1)
                    for k in range(SUB):
                        nc.vector.max_index(out=best_at[:, k], in_max=best[:, k], in_values=logits[:, k]).then_inc(step, 1)
                if part == 2:
                    dve.wait_ge(step, done + 10)
                    nc.vector.tensor_copy(at[:], best_at[:, :, 0:2]).then_inc(step, 1)
                    dve.wait_ge(ratio_ready, j + 1)
                    nc.vector.tensor_scalar(denom[:], ratio[:], 1.0, None, ALU.add).then_inc(step, 1)
                    dve.wait_ge(step, done + 12)
                    nc.vector.reciprocal(share[:, :, 0], denom[:]).then_inc(step, 1)
                    for r in range(2):
                        nc.vector.tensor_tensor(hot[:, r], w["index"][:].unsqueeze(1).to_broadcast(lanes),
                                                at[:, :, r:r + 1].to_broadcast(lanes), ALU.is_equal).then_inc(step, 1)
                    dve.wait_ge(step, done + 13)
                    nc.vector.tensor_tensor(share[:, :, 1], ratio[:], share[:, :, 0], ALU.mult).then_inc(step, 1)
                if part == 3:
                    dve.wait_ge(step, done + 16)
                    for r in range(2):
                        nc.vector.tensor_tensor(hot[:, r], hot[:, r], share[:, :, r:r + 1].to_broadcast(lanes),
                                                ALU.mult).then_inc(step, 1)
                    dve.wait_ge(step, done + 18)
                    nc.vector.tensor_tensor(gates[:, slot], hot[:, 0], hot[:, 1], ALU.add).then_inc(step, 1)

            dve.sem_inc(scaled_ready, 2)
            dve.sem_inc(added, 1)
            for part in range(4):
                router(0, 0, part, first=True)
            with dve.Fori(0, TILES // 2) as i:
                for slot in range(2):
                    j = 2 * i + slot
                    dve.wait_ge(step, ROUTER * (j + 1))
                    for k in range(SUB):
                        dve.wait_ge(expert_ready, SUB * j + k + 1)
                        if k == 1:
                            dve.wait_ge(step, ROUTER * (j + 1) + 1)
                        nc.vector.tensor_tensor(scaled[:, k % 2], expert_bank[:, k % 2],
                                                gates[:, slot, k].unsqueeze(2).to_broadcast([C, EXPERTS, C]),
                                                ALU.mult).then_inc(scaled_ready, 1)
                        router(j + 1, 1 - slot, k)
                        dve.wait_ge(scaled_ready, SUB * j + k + 3)
                        if k == 0:
                            dve.wait_ge(added, j + 1)
                        nc.vector.tensor_reduce(mixed[:, k], scaled[:, k % 2].rearrange("p e c -> p c e"), AX.X,
                                                ALU.add).then_inc(mixed_ready, 1)
                    dve.wait_ge(back, SUB * (j + 1))
                    tile = x[:, bass.ds(i * 2 * NT + slot * NT, NT)]
                    nc.vector.tensor_tensor(tile, tile, out_bank[:], ALU.add).then_inc(added, 1)


KERNEL = 9
EDGE = KERNEL // 2
PASSES = (("h", 1), ("h", -1), ("w", 1), ("w", -1))


def sweep_stage(nc, tag, w, a):
    with ExitStack() as ctx:
        s = Scope(nc, ctx, tag)
        run = s.sb("run", [C, 2, IMG, SIDE + 2 * EDGE])
        neg_b = s.sb("neg_b", [C, 4])
        bank = s.ps("bank", [C, 2, NT])
        ready = s.sem("ready")
        convolved = s.sem("convolved")
        placed = s.sem("placed")
        biased = s.sem("biased")
        block = ctx.enter_context(nc.Block())
        view = a.rearrange("c (b h w) -> c b h w", b=IMG, h=SIDE)
        G = IMG // 2

        def slices(axis, at, images=slice(0, IMG)):
            return view[:, images, at, :] if axis == "h" else view[:, images, :, at]

        def line(axis, at, g):
            images = slice(g * G, (g + 1) * G)
            if axis == "h":
                return view[:, images, bass.ds(at, 1), :].rearrange("c b o w -> c b (o w)")
            return view[:, images, :, bass.ds(at, 1)].rearrange("c b h o -> c b (h o)")

        steps = [SIDE - 1 if d > 0 else SIDE - 2 for _, d in PASSES]
        made = [2 * (sum(steps[:k]) + k) for k in range(4)]
        done = [2 * sum(steps[:k]) for k in range(4)]

        def each_step(eng, k, do):
            d = PASSES[k][1]
            first = 1 if d > 0 else SIDE - 2
            with eng.Fori(0, steps[k] // 2) as i:
                for r in range(2):
                    do(2 * i + r, r, 2 * i + (first + r) if d > 0 else i * -2 + (first - r))
            if steps[k] % 2:
                t = steps[k] - 1
                do(t, t % 2, first + d * t)

        @block.tensor
        def _(pe):
            for k in range(4):
                def conv(t, slot, at, k=k):
                    for g in range(2):
                        pe.wait_ge(ready, made[k] + 2 * t + g + 1)
                        for j in range(KERNEL):
                            mm = nc.tensor.matmul(bank[:, g, 0:G * SIDE], w["sweep"][:, k, j],
                                                  run[:, slot, g * G:(g + 1) * G, j:j + SIDE],
                                                  start=(j == 0), stop=(j == KERNEL - 1))
                        mm.then_inc(convolved, 1)

                each_step(pe, k, conv)

        @block.vector
        def _(dve):
            nc.vector.memset(run[:], 0.0).then_inc(biased, 1)
            nc.vector.tensor_scalar(neg_b[:], w["sweep_b"][:], -1.0, None, ALU.mult).then_inc(biased, 1)
            dve.sem_inc(placed, 4)
            for k, (axis, d) in enumerate(PASSES):
                dve.wait_ge(placed, 4 + done[k])
                dve.wait_ge(biased, 2 + k)
                last = SIDE if d > 0 else SIDE - 1
                swept = slices(axis, slice(1, last))
                nc.vector.tensor_scalar(swept, swept, w["sweep_b"][:, k:k + 1], None, ALU.add).then_inc(biased, 1)
                for g in range(2):
                    images = slice(g * G, (g + 1) * G)
                    nc.vector.tensor_copy(run[:, 0, images, EDGE:EDGE + SIDE],
                                          slices(axis, 0 if d > 0 else SIDE - 1, images)).then_inc(ready, 1)
                dve.wait_ge(biased, 3 + k)

                def finish(t, slot, at, k=k, axis=axis):
                    for g in range(2):
                        dve.wait_ge(placed, done[k] + 2 * t + g + 1)
                        dve.wait_ge(convolved, done[k] + 2 * t + g + 1)
                        nc.vector.scalar_tensor_tensor(
                            out=run[:, 1 - slot, g * G:(g + 1) * G, EDGE:EDGE + SIDE],
                            in0=bank[:, g, 0:G * SIDE].rearrange("c (b l) -> c b l", b=G), scalar=neg_b[:, k:k + 1],
                            in1=line(axis, at, g), op0=ALU.max, op1=ALU.add).then_inc(ready, 1)

                each_step(dve, k, finish)

        @block.scalar
        def _(act):
            for k, (axis, d) in enumerate(PASSES):
                def place(t, slot, at, k=k, axis=axis):
                    for g in range(2):
                        act.wait_ge(ready, made[k] + 2 * t + g + 3)
                        nc.scalar.activation(line(axis, at, g), run[:, 1 - slot, g * G:(g + 1) * G, EDGE:EDGE + SIDE],
                                             ACT.Copy).then_inc(placed, 1)

                each_step(act, k, place)


def add_stage(nc, tag, x, y):
    with ExitStack() as ctx:
        s = Scope(nc, ctx, tag)
        added = s.sem("added")
        block = ctx.enter_context(nc.Block())

        @block.vector
        def _(dve):
            nc.vector.tensor_tensor(x, x, y, ALU.add).then_inc(added, 1)
            dve.wait_ge(added, 1)


FILTERS = 16
QS = 2 * FILTERS
BLOCKS = LEN // 128
FREQS = BLOCKS
PLANES = 2 * FREQS


def choice_stage(nc, tag, w):
    with ExitStack() as ctx:
        s = Scope(nc, ctx, tag)
        logit = s.sb("logit", [C, 4])
        top = s.sb("top", [C, 1])
        soft = s.sb("soft", [C, 4])
        total = s.sb("total", [C, 1])
        hard = s.sb("hard", [C, 4])
        left = s.sb("left", [C, 4])
        parts = s.sb("parts", [C, 4])
        root = s.sb("root", [C, 1])
        step = s.sem("step")
        raised = s.sem("raised")
        rooted = s.sem("rooted")
        block = ctx.enter_context(nc.Block())
        weight, segment, sigma4 = w["weight"], w["segment"], w["sigma4"]

        @block.scalar
        def _(act):
            act.wait_ge(step, 3)
            nc.scalar.activation(soft[:], logit[:], ACT.Exp).then_inc(raised, 1)
            nc.scalar.activation(root[:], w["sigma"][:], ACT.Sqrt).then_inc(rooted, 1)
            act.wait_ge(rooted, 1)
            nc.scalar.activation(sigma4[:], root[:], ACT.Sqrt).then_inc(rooted, 1)

        @block.vector
        def _(dve):
            count = 0

            def do(instruction):
                nonlocal count
                count += 1
                instruction.then_inc(step, 1)
                dve.wait_ge(step, count)

            do(nc.vector.tensor_tensor(logit[:], w["log_weights"][:], w["gumbel"][:], ALU.add))
            do(nc.vector.tensor_reduce(top[:], logit[:], AX.X, ALU.max))
            do(nc.vector.tensor_scalar(logit[:], logit[:], top[:, 0:1], None, ALU.subtract))
            dve.wait_ge(raised, 1)
            do(nc.vector.tensor_reduce(total[:], soft[:], AX.X, ALU.add))
            do(nc.vector.reciprocal(total[:], total[:]))
            do(nc.vector.tensor_scalar(soft[:], soft[:], total[:, 0:1], None, ALU.mult))
            do(nc.vector.tensor_reduce(top[:], soft[:], AX.X, ALU.max))
            do(nc.vector.tensor_scalar(hard[:], soft[:], top[:, 0:1], None, ALU.is_ge))
            do(nc.vector.tensor_scalar(parts[:], hard[:], -1.0, 1.0, ALU.mult, ALU.add))
            do(nc.vector.memset(left[:], 1.0))
            for k in range(1, 4):
                do(nc.vector.tensor_tensor(left[:, k:k + 1], left[:, k - 1:k], parts[:, k - 1:k], ALU.mult))
            do(nc.vector.tensor_tensor(hard[:], hard[:], left[:], ALU.mult))
            do(nc.vector.tensor_tensor(weight[:], hard[:], soft[:], ALU.subtract))
            do(nc.vector.tensor_tensor(weight[:], weight[:], soft[:], ALU.add))
            for k in range(4):
                do(nc.vector.tensor_reduce(segment[:, k:k + 1], hard[:, 0:4 - k], AX.X, ALU.add))
            do(nc.vector.tensor_tensor(w["block_mask"][:], w["segment_of"][:], segment[0:64, :], ALU.mult))
            do(nc.vector.tensor_reduce(w["mask_col"][:], w["block_mask"][:], AX.X, ALU.add))
            do(nc.vector.tensor_scalar(w["m_u"][:], w["m_u_all"][:, 0], weight[:, 0:1], None, ALU.mult))
            for k in range(1, 4):
                do(nc.vector.scalar_tensor_tensor(out=w["m_u"][:], in0=w["m_u_all"][:, k], scalar=weight[:, k:k + 1],
                                                  in1=w["m_u"][:], op0=ALU.mult, op1=ALU.add))


def autoregressive_stage(nc, tag, w, u, x):
    TILES = LEN // NT
    with ExitStack() as ctx:
        s = Scope(nc, ctx, tag)
        bank = s.ps("bank", [C, 4, NT])
        summed = s.sem("summed")
        added = s.sem("added")
        block = ctx.enter_context(nc.Block())

        @block.tensor
        def _(pe):
            with pe.Fori(0, IMG) as b:
                for t in range(TILES):
                    pe.wait_ge(added, TILES * b + t + 1)
                    for i in range(3):
                        cut = i if t == 0 else 0
                        mm = nc.tensor.matmul(bank[:, t % 4, cut:NT], w["m_u"][:, i],
                                              u[:, bass.ds(b * LEN + (t * NT - i + cut), NT - cut)],
                                              start=(i == 0), stop=(i == 2), skip_group_check=True)
                    mm.then_inc(summed, 1)

        @block.vector
        def _(dve):
            dve.sem_inc(added, 4)
            with dve.Fori(0, IMG) as b:
                for t in range(TILES):
                    dve.wait_ge(summed, TILES * b + t + 1)
                    tile = x[:, bass.ds(b * LEN + t * NT, NT)]
                    k = (0, 1, 2, 2, 3, 3, 3, 3)[t]
                    nc.vector.scalar_tensor_tensor(out=tile, in0=bank[:, t % 4], scalar=w["segment"][:, k:k + 1],
                                                   in1=tile, op0=ALU.mult, op1=ALU.add).then_inc(added, 1)


def turn_stage(nc, tag, consts, u, x, turned_dram, x_dram):
    with ExitStack() as ctx:
        s = Scope(nc, ctx, tag)
        out = s.sb("out", [C, 4, 4, C])
        staged = s.sb("staged", [C, 4, NT])
        bank = s.ps("bank", [C, 4, 4, C])
        staged_ready = s.sem("staged_ready")
        turned = s.sem("turned")
        copied = s.sem("copied")
        stored = [s.sem(f"stored{t}") for t in range(4)]
        x_stored = s.sem("x_stored")
        block = ctx.enter_context(nc.Block())
        steps = TOK // QUAD

        @block.sync
        def _(sp):
            sp.dma_start(x_dram, x).then_inc(x_stored, 16)
            with sp.Fori(0, steps) as i:
                for t in range(4):
                    sp.wait_ge(copied, 4 * i + t + 5)
                    rows = turned_dram[bass.ds(i * QUAD + t * NT, NT), :].rearrange("(k p) c -> p k c", p=128)
                    sp.dma_start(rows, out[:, t]).then_inc(stored[t], 16)
            for t in range(4):
                sp.wait_ge(stored[t], 16 * (steps + 1))
            sp.wait_ge(x_stored, 16)

        @block.tensor
        def _(pe):
            with pe.Fori(0, steps) as i:
                for t in range(4):
                    pe.wait_ge(staged_ready, 4 * i + t + 1)
                    pe.wait_ge(copied, 4 * i + t + 1)
                    for k in range(4):
                        mm = nc.tensor.matmul(bank[:, t, k], staged[:, t, 128 * k:128 * (k + 1)], consts["ident"][:],
                                              start=True, stop=True)
                    mm.then_inc(turned, 1)

        @block.scalar
        def _(act):
            with act.Fori(0, steps) as i:
                for t in range(4):
                    act.wait_ge(copied, 4 * i + t + 1)
                    nc.scalar.activation(staged[:, t], u[:, bass.ds(i * QUAD + t * NT, NT)],
                                         ACT.Copy).then_inc(staged_ready, 1)

        @block.vector
        def _(dve):
            dve.sem_inc(copied, 4)
            for t in range(4):
                dve.sem_inc(stored[t], 16)
            with dve.Fori(0, steps) as i:
                for t in range(4):
                    dve.wait_ge(turned, 4 * i + t + 1)
                    dve.wait_ge(stored[t], 16 * i + 16)
                    nc.vector.tensor_copy(out[:, t], bank[:, t]).then_inc(copied, 1)


def filters_stage(nc, tag, w, phi_dram):
    with ExitStack() as ctx:
        s = Scope(nc, ctx, tag)
        taps = s.sb("taps", [BLOCKS, FILTERS, 128])
        table = s.sb("table", [C, FREQS, 3, 128])
        inner = s.sb("inner", [C, PLANES, 3 * QS])
        out = s.sb("out", [3 * QS, FREQS, 2 * 128], F32R)
        blocks_bank = s.ps("blocks_bank", [C, FILTERS, PLANES])
        bank = s.ps("bank", [C, 4, NT])
        loaded = s.sem("loaded")
        tables_loaded = s.sem("tables_loaded")
        transformed = s.sem("transformed")
        spread = s.sem("spread")
        made = s.sem("made")
        rounded = s.sem("rounded")
        split = s.sem("split")
        stored = s.sem("stored")
        block = ctx.enter_context(nc.Block())

        @block.sync
        def _(sp):
            sp.dma_start(taps[:], w["phi"]).then_inc(loaded, 16)
            sp.dma_start(table[:], w["forward"].rearrange("f t k n -> t f k n")).then_inc(tables_loaded, 16)
            sp.wait_ge(split, FREQS)
            sp.dma_start(phi_dram.rearrange("f q n -> q f n"), out[:].bitcast(F32)).then_inc(stored, 16)
            sp.wait_ge(stored, 16)

        @block.tensor
        def _(pe):
            pe.wait_ge(loaded, 16)
            for k in range(FILTERS):
                mm = nc.tensor.matmul(blocks_bank[:, k], taps[:, k], w["dft_taps"][:], start=True, stop=True)
            mm.then_inc(transformed, 1)
            pe.wait_ge(tables_loaded, 16)
            pe.wait_ge(spread, 6)
            for f in range(FREQS):
                if f >= 4:
                    pe.wait_ge(split, f - 3)
                dst = bank[0:3 * QS, f % 4, 0:256]
                nc.tensor.matmul(dst, inner[:, 2 * f], table[:, f, 1:3], start=True, stop=False)
                nc.tensor.matmul(dst, inner[:, 2 * f + 1], table[:, f, 0:2], start=False, stop=True).then_inc(made, 1)

        @block.scalar
        def _(act):
            for f in range(FREQS):
                act.wait_ge(made, f + 1)
                nc.scalar.activation(out[:, f], bank[0:3 * QS, f % 4, 0:256], ACT.Copy).then_inc(rounded, 1)

        @block.vector
        def _(dve):
            dve.wait_ge(transformed, 1)
            by_plane = blocks_bank[:].rearrange("t k p -> t p k")
            for copy in range(3):
                nc.vector.tensor_copy(inner[:, :, QS * copy:QS * copy + FILTERS], by_plane).then_inc(spread, 1)
                nc.vector.tensor_scalar(inner[:, :, QS * copy + FILTERS:QS * (copy + 1)], by_plane,
                                        w["alternate"][:, 0:1], None, ALU.mult).then_inc(spread, 1)
            low = slice(2 * QS, 3 * QS)
            for f in range(FREQS):
                dve.wait_ge(rounded, f + 1)
                nc.vector.tensor_tensor(out[low, f], bank[low, f % 4, 0:256], out[low, f].bitcast(F32),
                                        ALU.subtract).then_inc(split, 1)


def forward_stage(nc, tag, w, turned_dram, uhat_dram):
    FREE = 32 * C
    with ExitStack() as ctx:
        s = Scope(nc, ctx, tag)
        rows = s.sb("rows", [C, 2, FREE])
        out = s.sb("out", [C, 2, FREE])
        bank = s.ps("bank", [C, 8, NT])
        loaded = [s.sem(f"loaded{k}") for k in range(2)]
        transformed = s.sem("transformed")
        copied_a = s.sem("copied_a")
        copied_d = s.sem("copied_d")
        stored = [s.sem(f"stored{k}") for k in range(2)]
        block = ctx.enter_context(nc.Block())
        src = turned_dram.rearrange("(b p n) c -> p b (n c)", b=IMG, p=128)
        T = FREE // NT

        @block.sync
        def _(sp):
            def load(b):
                sp.dma_start(rows[:, b % 2], src[:, b]).then_inc(loaded[b % 2], 16)

            load(0)
            load(1)
            for n in range(2 * IMG):
                b, half = n // 2, n % 2
                sp.wait_ge(copied_a, T // 2 * (n + 1))
                sp.wait_ge(copied_d, T // 2 * (n + 1))
                dst = uhat_dram[PLANES // 2 * half:PLANES // 2 * (half + 1), b].rearrange("p (x n) c -> p x (n c)", x=4)
                sp.dma_start(dst, out[:, half]).then_inc(stored[half], 16)
                if half == 1 and b + 2 < IMG:
                    load(b + 2)
            for half in range(2):
                sp.wait_ge(stored[half], 16 * IMG)

        @block.tensor
        def _(pe):
            for n in range(2 * IMG):
                b, half = n // 2, n % 2
                if half == 0:
                    pe.wait_ge(loaded[b % 2], 16 * (b // 2 + 1))
                for t in range(T):
                    m = n * T + t
                    if m >= 8:
                        pe.wait_ge(copied_d if t % 2 else copied_a, (m - 8) // 2 + 1)
                    nc.tensor.matmul(bank[:, m % 8], w["dft"][:, half], rows[:, b % 2, NT * t:NT * (t + 1)],
                                     start=True, stop=True).then_inc(transformed, 1)

        @block.scalar
        def _(act):
            for n in range(2 * IMG):
                for t in range(0, T, 2):
                    m = n * T + t
                    act.wait_ge(transformed, m + 1)
                    if n >= 2:
                        act.wait_ge(stored[n % 2], 16 * (n // 2))
                    nc.scalar.activation(out[:, n % 2, NT * t:NT * (t + 1)], bank[:, m % 8],
                                         ACT.Copy).then_inc(copied_a, 1)

        @block.vector
        def _(dve):
            for n in range(2 * IMG):
                for t in range(1, T, 2):
                    m = n * T + t
                    dve.wait_ge(transformed, m + 1)
                    if n >= 2:
                        dve.wait_ge(stored[n % 2], 16 * (n // 2))
                    nc.vector.tensor_copy(out[:, n % 2, NT * t:NT * (t + 1)], bank[:, m % 8]).then_inc(copied_d, 1)


def matrices_stage(nc, tag, w, m_stack):
    CHUNK = 4 * NT
    CHUNKS = C * C // CHUNK
    with ExitStack() as ctx:
        s = Scope(nc, ctx, tag)
        raw = s.sb("raw", [C, 2, CHUNK])
        of_branch = s.sb("of_branch", [C, 4])
        factor = s.sb("factor", [C, 1])
        combine = s.sb("combine", [C, 3 * QS])
        bank = s.ps("bank", [C, 4, NT])
        loaded = [s.sem(f"loaded{k}") for k in range(2)]
        step = s.sem("step")
        combined = s.sem("combined")
        rounded = s.sem("rounded")
        split = s.sem("split")
        block = ctx.enter_context(nc.Block())
        flat = m_stack[:].rearrange("q e d -> q (e d)")
        TILES = CHUNK // NT

        @block.sync
        def _(sp):
            for c in range(CHUNKS):
                if c >= 2:
                    sp.wait_ge(combined, TILES * (c - 1))
                sp.dma_start(raw[:, c % 2], w["m_all"][:, CHUNK * c:CHUNK * (c + 1)]).then_inc(loaded[c % 2], 16)

        @block.tensor
        def _(pe):
            pe.wait_ge(step, 4)
            for c in range(CHUNKS):
                pe.wait_ge(loaded[c % 2], 16 * (c // 2 + 1))
                for t in range(TILES):
                    if c:
                        pe.wait_ge(split, TILES * (c - 1) + t + 1)
                    nc.tensor.matmul(bank[0:3 * QS, t], combine[:], raw[:, c % 2, NT * t:NT * (t + 1)],
                                     start=True, stop=True).then_inc(combined, 1)

        @block.scalar
        def _(act):
            for n in range(CHUNKS * TILES):
                act.wait_ge(combined, n + 1)
                nc.scalar.activation(flat[:, NT * n:NT * (n + 1)], bank[0:3 * QS, n % TILES],
                                     ACT.Copy).then_inc(rounded, 1)

        @block.vector
        def _(dve):
            nc.vector.tensor_tensor(of_branch[:], w["branch_of"][:], w["weight"][:], ALU.mult).then_inc(step, 1)
            dve.wait_ge(step, 1)
            nc.vector.tensor_reduce(factor[:], of_branch[:], AX.X, ALU.add).then_inc(step, 1)
            dve.wait_ge(step, 2)
            nc.vector.tensor_tensor(factor[:], factor[:], w["sigma4"][:], ALU.mult).then_inc(step, 1)
            dve.wait_ge(step, 3)
            nc.vector.tensor_scalar(combine[:], w["filter_of"][:], factor[:, 0:1], None, ALU.mult).then_inc(step, 1)
            for n in range(CHUNKS * TILES):
                dve.wait_ge(rounded, n + 1)
                cols = slice(NT * n, NT * (n + 1))
                nc.vector.tensor_tensor(flat[0:QS, cols], bank[0:QS, n % TILES], flat[0:QS, cols].bitcast(F32),
                                        ALU.subtract).then_inc(split, 1)


def spectral_stage(nc, tag, w, m_stack, phi_dram, uhat_dram, y_dram, yhat_dram):
    HALF = 64
    GROUPS = HALF // 4
    BUILD = 8
    BUILDS = C // BUILD
    PARTS = 2 * IMG
    with ExitStack() as ctx:
        s = Scope(nc, ctx, tag)
        g = s.sb("g", [C, 2, 2, HALF, C])
        phi = s.sb("phi", [3 * QS, 2, 2, HALF], F32R)
        a = s.sb("a", [C, PARTS, C])
        fwd = s.sb("fwd", [C, 3, C])
        inv = s.sb("inv", [C, 3, C])
        x = s.sb("x", [C, 2, HALF, 3 * IMG])
        y = s.sb("y", [C, 2, GROUPS // 2, C])
        y_t = s.sb("y_t", [C, PARTS, C])
        z = s.sb("z", [C, 2, IMG, C])
        g_bank = s.ps("g_bank", [C, 2, BUILD, 2, HALF])
        y_bank = s.ps("y_bank", [C, 2, 4, C])
        x_bank = s.ps("x_bank", [C, IMG, 2, HALF])
        z_bank = s.ps("z_bank", [C, 2, 2, C])
        phi_loaded = [s.sem(f"phi_loaded{h}") for h in range(2)]
        a_loaded = s.sem("a_loaded")
        inv_loaded = s.sem("inv_loaded")
        built = s.sem("built")
        g_act = s.sem("g_act")
        g_dve = s.sem("g_dve")
        applied = s.sem("applied")
        y_copied = s.sem("y_copied")
        y_moved = [s.sem(f"y_moved{k}") for k in range(2)]
        padded = s.sem("padded")
        y_loaded = s.sem("y_loaded")
        x_made = s.sem("x_made")
        x_ready = s.sem("x_ready")
        z_made = s.sem("z_made")
        z_copied = s.sem("z_copied")
        z_stored = s.sem("z_stored")
        zeroed = s.sem("zeroed")
        block = ctx.enter_context(nc.Block())
        G_HALF = BUILDS // 2

        @block.sync
        def _(sp):
            def load_phi(i, n, h, first=False):
                if not first:
                    sp.wait_ge(built, BUILDS * (n - 1))
                src = phi_dram[bass.ds(i, 1)].rearrange("o q (r f) -> (o q) r f", r=2)[:, :, HALF * h:HALF * (h + 1)]
                sp.dma_start(phi[:, h].bitcast(F32), src).then_inc(phi_loaded[h], 16)

            def load_a(i, first=False):
                if not first:
                    sp.wait_ge(x_made, 2 * i)
                sp.dma_start(a[:], uhat_dram[bass.ds(2 * i, 2)].rearrange("r b t c -> t (r b) c")).then_inc(a_loaded, 16)
                sp.dma_start(fwd[:], w["forward"][bass.ds(i, 1)].rearrange("o t k n -> (o t) k n")).then_inc(a_loaded, 16)

            def move_y(i, n, k, half):
                sp.wait_ge(y_copied, 4 * n + 2 * k + 4)
                for tile in range(4):
                    row = HALF * half + GROUPS * tile + GROUPS // 2 * k
                    dst = y_dram[bass.ds(i, 1), row:row + GROUPS // 2].rearrange("o g r e -> r (o g) e")
                    sp.dma_start(dst, y[32 * tile:32 * tile + PARTS, k]).then_inc(y_moved[k], 16)

            def wait_y(i):
                for k in range(2):
                    sp.wait_ge(y_moved[k], 64 * (2 * i + 2))

            def load_y(i):
                sp.dma_start(y_t[:], y_dram[bass.ds(i, 1)].rearrange("o f r e -> (o f) r e")).then_inc(y_loaded, 16)

            def load_inv(i):
                sp.wait_ge(z_made, 2 * i + 2)
                sp.dma_start(inv[:], w["backward"][bass.ds(i, 1)].rearrange("o t k n -> (o t) k n")).then_inc(inv_loaded, 16)

            def store_z(i):
                sp.wait_ge(z_copied, 2 * i + 3)
                sp.dma_start(yhat_dram[bass.ds(2 * i, 2)].rearrange("r e n -> e r n"),
                             z[:].rearrange("e r b t -> e r (b t)")).then_inc(z_stored, 16)

            def each(i, last=False):
                load_inv(i)
                for k in range(2):
                    move_y(i, 2 * i, k, 1)
                wait_y(i)
                if not last:
                    load_phi(i + 1, 2 * i + 2, 0)
                load_y(i)
                move_y(i + 1, 2 * i + 1, 0, 0)
                if not last:
                    load_a(i + 1)
                store_z(i)
                move_y(i + 1, 2 * i + 1, 1, 0)
                if not last:
                    load_phi(i + 1, 2 * i + 3, 1)

            sp.wait_ge(zeroed, 3)
            sp.dma_start(y_dram[0, 0:HALF], g[0:HALF, 1, 0, 0:PARTS]).then_inc(padded, 16)
            load_phi(0, 0, 0, first=True)
            load_a(0, first=True)
            load_phi(0, 1, 1, first=True)
            sp.wait_ge(padded, 16)
            with sp.Fori(0, FREQS - 1) as i:
                each(i)
            each(FREQS - 1, last=True)
            load_inv(FREQS)
            for k in range(2):
                move_y(FREQS, 2 * FREQS, k, 1)
            wait_y(FREQS)
            load_y(FREQS)
            store_z(FREQS)
            sp.wait_ge(z_stored, 16 * (FREQS + 2))

        @block.tensor
        def _(pe):
            def apply(n, half, c):
                if c == 0:
                    pe.wait_ge(g_act, G_HALF * n + 1)
                    pe.wait_ge(g_dve, G_HALF * n + 1)
                    pe.wait_ge(x_ready, n + 1)
                if c % 4 == 0:
                    pe.wait_ge(y_copied, 4 * n + c // 4 + 1)
                for part in range(2):
                    for tile in range(4):
                        f = GROUPS * tile + c
                        first = (1 - part) * IMG
                        mm = nc.tensor.matmul(y_bank[32 * tile:32 * tile + PARTS, c // 4 % 2, c % 4],
                                              x[:, half, f, first:first + PARTS], g[:, half, part, f],
                                              start=(part == 0), stop=(part == 1), skip_group_check=True)
                mm.then_inc(applied, 1)

            def forward(i, n, h):
                if h == 0:
                    pe.wait_ge(a_loaded, 32 * i + 32)
                pe.wait_ge(x_ready, n + 1)
                for b in range(IMG):
                    cols = slice(HALF * h, HALF * (h + 1))
                    nc.tensor.matmul(x_bank[:, b], a[:, b], fwd[:, 1:3, cols], start=True, stop=False)
                    mm = nc.tensor.matmul(x_bank[:, b], a[:, IMG + b], fwd[:, 0:2, cols], start=False, stop=True)
                mm.then_inc(x_made, 1)

            def backward(i, pair):
                if pair == 0:
                    pe.wait_ge(inv_loaded, 16 * i + 16)
                    pe.wait_ge(y_loaded, 16 * i + 16)
                pe.wait_ge(z_copied, 2 * i + pair + 1)
                for b in range(2):
                    nc.tensor.matmul(z_bank[:, b], y_t[:, 2 * pair + b], inv[:, 1:3], start=True, stop=False)
                    mm = nc.tensor.matmul(z_bank[:, b], y_t[:, IMG + 2 * pair + b], inv[:, 0:2], start=False, stop=True)
                mm.then_inc(z_made, 1)

            pe.wait_ge(zeroed, 4)
            with pe.Fori(0, FREQS) as i:
                for h in range(2):
                    n = 2 * i + h
                    pe.wait_ge(phi_loaded[h], 16 * i + 16)
                    for c in range(BUILDS):
                        pe.wait_ge(g_dve if c % 2 else g_act, G_HALF * n + c // 2 + 1)
                        for e in range(BUILD):
                            mm = nc.tensor.matmul(g_bank[:, c % 2, e], m_stack[:, BUILD * c + e], phi[:, h],
                                                  start=True, stop=True)
                        mm.then_inc(built, 1)
                        apply(n, 1 - h, c)
                        if c == 1:
                            forward(i, n, h)
                        if h == 1 and c in (4, 7):
                            backward(i, c // 7)
            for c in range(GROUPS):
                apply(2 * FREQS, 1, c)
            for pair in range(2):
                backward(FREQS, pair)

        def copy_g(eng, copy, n, h, c, ready):
            if c < 2:
                eng.wait_ge(applied, GROUPS * n + 16)
            eng.wait_ge(built, BUILDS * n + c + 1)
            copy(g[:, h, :, :, BUILD * c:BUILD * (c + 1)].rearrange("d r f e -> d (r f) e"),
                 g_bank[:, c % 2].rearrange("d e r f -> d (r f) e")).then_inc(ready, 1)

        @block.scalar
        def _(act):
            def copy_y(n, j):
                act.wait_ge(applied, GROUPS * n + 4 * j + 20)
                if j % 2 == 0:
                    act.wait_ge(y_moved[j // 2], 64 * n + 64)
                nc.scalar.activation(y[:, j // 2, 4 * (j % 2):4 * (j % 2) + 4], y_bank[:, j % 2],
                                     ACT.Copy).then_inc(y_copied, 1)

            act.wait_ge(zeroed, 4)
            with act.Fori(0, FREQS) as i:
                for h in range(2):
                    n = 2 * i + h
                    for c in range(0, BUILDS, 2):
                        copy_g(act, lambda out, src: nc.scalar.activation(out, src, ACT.Copy), n, h, c, g_act)
                        if c % 4 == 2:
                            copy_y(n, c // 4)
            for j in range(4):
                copy_y(2 * FREQS, j)

        @block.vector
        def _(dve):
            def copy_x(n, h):
                dve.wait_ge(x_made, n + 1)
                nc.vector.tensor_copy(x[:, h, :, IMG:].rearrange("c f (r b) -> c f r b", r=2),
                                      x_bank[:].rearrange("c b r f -> c f r b"))
                nc.vector.tensor_scalar(x[:, h, :, 0:IMG], x_bank[:, :, 1].rearrange("c b f -> c f b"), -1.0, None,
                                        ALU.mult).then_inc(x_ready, 1)

            def copy_z(i, pair):
                dve.wait_ge(z_made, 2 * i + pair + 3)
                if pair == 0:
                    dve.wait_ge(z_stored, 16 * i + 16)
                nc.vector.tensor_copy(z[:, :, 2 * pair:2 * pair + 2].rearrange("e r b t -> e b r t"),
                                      z_bank[:]).then_inc(z_copied, 1)

            for buffer in (g[:, 1], x[:], y_t[:], y_bank[:]):
                nc.vector.memset(buffer, 0.0).then_inc(zeroed, 1)
            dve.wait_ge(zeroed, 4)
            for sem, credit in ((g_act, 1), (g_dve, 1), (applied, 16), (y_copied, 2), (y_moved[0], 64),
                                (y_moved[1], 64), (x_ready, 1), (z_made, 2), (z_copied, 1), (z_stored, 16)):
                dve.sem_inc(sem, credit)
            with dve.Fori(0, FREQS) as i:
                for h in range(2):
                    n = 2 * i + h
                    for c in range(1, BUILDS, 2):
                        copy_g(dve, nc.vector.tensor_copy, n, h, c, g_dve)
                        if c == 3:
                            copy_x(n, h)
                        if h == 1 and c in (5, 9):
                            copy_z(i, c // 9)
            for pair in range(2):
                copy_z(FREQS, pair)


def inverse_stage(nc, tag, w, yhat_dram, x_dram, out_dram):
    X = 2
    CH = 8
    CHUNKS = C // X // CH
    OUT = X * BLOCKS
    with ExitStack() as ctx:
        s = Scope(nc, ctx, tag)
        rows = s.sb("rows", [C, 2, CH, NT])
        x = s.sb("x", [OUT, 2, CH, IMG, 128])
        bank = s.ps("bank", [C, 8, NT])
        rows_loaded = [s.sem(f"rows_loaded{k}") for k in range(2)]
        x_loaded = [s.sem(f"x_loaded{k}") for k in range(2)]
        transformed = s.sem("transformed")
        added = s.sem("added")
        stored = [s.sem(f"stored{k}") for k in range(2)]
        block = ctx.enter_context(nc.Block())
        N = CH

        def by_block(dram, chunk, xx):
            rows_of = dram[C // X * xx + CH * chunk:C // X * xx + CH * (chunk + 1), :]
            return rows_of.rearrange("c (b j t) -> j (c b) t", b=IMG, j=BLOCKS)

        @block.sync
        def _(sp):
            def load(c):
                if c >= 2:
                    sp.wait_ge(transformed, N * (c - 1))
                src = yhat_dram[2:].rearrange("p (x e) n -> (p x) e n", x=X)[:, CH * c:CH * (c + 1)]
                sp.dma_start(rows[:, c % 2], src).then_inc(rows_loaded[c % 2], 16)
                if c >= 2:
                    sp.wait_ge(stored[c % 2], 16 * X * (c // 2))
                for xx in range(X):
                    sp.dma_start(x[BLOCKS * xx:BLOCKS * (xx + 1), c % 2].rearrange("j c b t -> j (c b) t"),
                                 by_block(x_dram, c, xx)).then_inc(x_loaded[c % 2], 16)

            load(0)
            load(1)
            for c in range(CHUNKS):
                sp.wait_ge(added, N * (c + 1))
                for xx in range(X):
                    sp.dma_start(by_block(out_dram, c, xx),
                                 x[BLOCKS * xx:BLOCKS * (xx + 1), c % 2].rearrange("j c b t -> j (c b) t")
                                 ).then_inc(stored[c % 2], 16)
                if c + 2 < CHUNKS:
                    load(c + 2)
            for slot in range(2):
                sp.wait_ge(stored[slot], 16 * X * CHUNKS // 2)

        @block.tensor
        def _(pe):
            for c in range(CHUNKS):
                pe.wait_ge(rows_loaded[c % 2], 16 * (c // 2 + 1))
                for k in range(N):
                    if c:
                        pe.wait_ge(added, N * (c - 1) + k + 1)
                    nc.tensor.matmul(bank[0:OUT, k], w["inverse"][:], rows[:, c % 2, k],
                                     start=True, stop=True).then_inc(transformed, 1)

        @block.vector
        def _(dve):
            for c in range(CHUNKS):
                dve.wait_ge(x_loaded[c % 2], 16 * X * (c // 2 + 1))
                for k in range(N):
                    dve.wait_ge(transformed, N * c + k + 1)
                    tile = x[:, c % 2, k]
                    nc.vector.scalar_tensor_tensor(out=tile, in0=bank[0:OUT, k].rearrange("p (b t) -> p b t", b=IMG),
                                                   scalar=w["mask_col"][:, 0:1], in1=tile, op0=ALU.mult,
                                                   op1=ALU.add).then_inc(added, 1)


def metaformer(nc, a, out):
    Scope.semaphores = []
    with ExitStack() as ctx:
        def scratch(name, shape, dt=F32):
            return nc.dram_tensor(name, shape, dt).ap()

        turned_dram = scratch("turned", [TOK, C])
        x_dram = scratch("x_kept", [C, TOK])
        uhat_dram = scratch("uhat", [PLANES, IMG, 128, C])
        yhat_dram = scratch("yhat", [2 + PLANES, C, NT])
        y_dram = scratch("y_within", [1 + FREQS, 128, 2 * IMG, C])
        phi_dram = scratch("phi_hat", [FREQS, 3 * QS, 2 * 128])

        def buffers(stack, names, tag="sb"):
            return {n: stack.enter_context(nc.sbuf_tensor(f"{tag}_{n}", list(a[n].shape), a[n].dtype)) for n in names}

        small = {n: ctx.enter_context(nc.sbuf_tensor(f"sb_{n}", shape, F32)) for n, shape in (
            ("weight", [C, 4]), ("segment", [C, 4]), ("sigma4", [C, 1]), ("mask_col", [64, 1]))}
        with ExitStack() as held:
            consts = buffers(held, ["ident", "mean"])
            load_stage(nc, "load_consts", [(consts[n][:], a[n]) for n in consts])
            wide = held.enter_context(nc.sbuf_tensor("wide", [C, PAD + TOK + PAD], F32))
            xh = wide[:, PAD:PAD + TOK]
            load_stage(nc, "load_x", [(xh, a["x"])])
            layernorm_stage(nc, "norm_c0", consts, xh, xh, 1e-6)
            layernorm_stage(nc, "norm_m0", consts, xh, xh, 1e-5)
            with ExitStack() as inner:
                names = ["order", "in", "x_proj", "dt_proj", "out_proj", "select", "less", "mask", "columns", "a_log",
                         "conv_w"]
                w = buffers(inner, names)
                load_stage(nc, "load_mamba", [(w[n][:], a[n]) for n in names])
                w["x"], w["dt"], w["out"] = w["x_proj"], w["dt_proj"], w["out_proj"]
                for n, first, count in COLUMNS:
                    w[n] = w["columns"][:, first:first + count]
                mamba_stage(nc, "mamba", consts, w, wide)
            with ExitStack() as inner:
                x = inner.enter_context(nc.sbuf_tensor("x_sb", [C, TOK], F32))
                w = buffers(inner, ["gamma", "beta", "w_p", "b_p"], tag="proj")
                load_stage(nc, "load_proj", [(x[:], a["x"])] + [(w[n][:], a[n]) for n in w])
                layernorm_stage(nc, "norm_m1", consts, xh, xh, 1e-5, gamma=w["gamma"][:, 0:1])
                project_stage(nc, "project", w, xh, x)
                layernorm_stage(nc, "norm_t0", consts, x, xh, 1e-5)
                with ExitStack() as moe:
                    names = ["router", "expert", "bias", "router_b", "index"]
                    w = buffers(moe, names)
                    load_stage(nc, "load_experts", [(w[n][:], a[n]) for n in names])
                    experts_stage(nc, "experts", consts, w, wide[:, PAD:], x)
                layernorm_stage(nc, "norm_c1", consts, x, xh, 1e-6)
                with ExitStack() as sweep:
                    w = buffers(sweep, ["sweep", "sweep_b"])
                    load_stage(nc, "load_sweep", [(w[n][:], a[n]) for n in w])
                    sweep_stage(nc, "sweep", w, xh)
                add_stage(nc, "add", x[:], xh)
                Scope.recycle(nc)
                layernorm_stage(nc, "norm_t1", consts, x, xh, 1e-5)
                with ExitStack() as ar:
                    names = ["log_weights", "gumbel", "sigma", "segment_of", "m_u_all"]
                    w = buffers(ar, names)
                    w.update(small)
                    w["block_mask"] = ar.enter_context(nc.sbuf_tensor("sb_block_mask", [64, 4], F32))
                    w["m_u"] = ar.enter_context(nc.sbuf_tensor("sb_m_u", [C, 3, C], F32))
                    load_stage(nc, "load_ar", [(w[n][:], a[n]) for n in names])
                    choice_stage(nc, "choice", w)
                    autoregressive_stage(nc, "ar", w, xh, x)
                turn_stage(nc, "turn", consts, xh, x[:], turned_dram, x_dram)
        with ExitStack() as inner:
            names = ["dft", "dft_taps", "alternate"]
            w = buffers(inner, names)
            load_stage(nc, "load_dft", [(w[n][:], a[n]) for n in names])
            filters_stage(nc, "filters", dict(w, phi=a["phi"], forward=a["forward"]), phi_dram)
            forward_stage(nc, "forward", w, turned_dram, uhat_dram)
        with ExitStack() as inner:
            m_stack = inner.enter_context(nc.sbuf_tensor("m_stack", [3 * QS, C, C], F32R))
            with ExitStack() as m:
                names = ["branch_of", "filter_of"]
                w = buffers(m, names)
                load_stage(nc, "load_matrices", [(w[n][:], a[n]) for n in names])
                matrices_stage(nc, "matrices", dict(small, m_all=a["m_all"], **w), m_stack)
            spectral_stage(nc, "spectral", a, m_stack, phi_dram, uhat_dram, y_dram, yhat_dram)
        with ExitStack() as inner:
            w = buffers(inner, ["inverse"])
            load_stage(nc, "load_inverse", [(w["inverse"][:], a["inverse"])])
            inverse_stage(nc, "inverse", dict(small, inverse=w["inverse"]), yhat_dram, x_dram, out)


def kernel(**inputs):
    import math

    import numpy as np
    from concourse import bacc
    from concourse.bass_utils import run_bass_kernel_spmd

    import ml_dtypes

    i = {k: np.asarray(v) for k, v in inputs.items()}
    m = {k[len("L0_conv_"):]: v for k, v in i.items() if k.startswith("L0_conv_")}
    h = INNER // 2

    def over_partitions(v, rows=C):
        return np.ascontiguousarray(np.broadcast_to(v[None], (rows, *v.shape)))

    def by_half(v):
        return np.ascontiguousarray(v.reshape(2, h, *v.shape[1:]).swapaxes(0, 1))

    order = np.zeros((C, 2, C), np.float32)
    for c in range(C):
        order[c, 0, c] = 1
        order[(c % 8) * 16 + c // 8, 1, c] = 1
    select = np.zeros((96, 2 * STATES, C), ml_dtypes.bfloat16)
    for k in range(96):
        select[k, k % 32] = 1
    less = np.zeros((96, 2), np.float32)
    less[32:, 0] = -1
    less[64:, 1] = -1
    mask = np.ones((C, PAIRS + 1), np.float32)
    mask[:, ::PAIRS // IMG] = 0

    def plane(p, j):
        angle = 2 * math.pi * (p // 2 + 0.25) * j / BLOCKS
        return -math.sin(angle) if p % 2 else math.cos(angle)

    planes = np.array([[plane(p, j) for p in range(PLANES)] for j in range(BLOCKS)])
    dft = np.zeros((BLOCKS, 4, 2, PLANES // 2, 4), np.float32)
    for x in range(4):
        dft[:, x, :, :, x] = planes.reshape(BLOCKS, 2, PLANES // 2)
    inverse = np.zeros((PLANES, 2, 2, BLOCKS), np.float32)
    for x in range(2):
        inverse[:, x, x, :] = planes.T / LEN
    f1, t, f2 = np.arange(FREQS)[:, None, None], np.arange(128)[:, None], np.arange(128)
    angle = 2 * math.pi * (f1 + 0.25 + FREQS * f2) * t / LEN
    sin, cos = np.sin(angle), np.cos(angle)
    forward = np.stack([sin, cos, -sin], 2).astype(np.float32)
    sin, cos = sin.swapaxes(1, 2), cos.swapaxes(1, 2)
    backward = np.stack([-sin, cos, sin], 2).astype(np.float32)
    backward = np.concatenate([backward[:1], backward])
    alternate = np.array([[1], [-1]] * (C // 2), np.float32)
    segment_of = np.zeros((64, 4), np.float32)
    for r in range(64):
        segment_of[r, sum(r % BLOCKS >= BLOCKS // edge for edge in (8, 4, 2))] = 1
    branch_of = np.repeat(np.eye(4, dtype=np.float32), QS, 0)
    filter_of = np.tile(np.eye(QS, dtype=np.float32), (4, 3))

    x_dbl = np.zeros((C, INNER), np.float32)
    rank = m["W_dt"].shape[1]
    for part in range(3):
        x_dbl[32 * part:32 * (part + 1)] = m["W_x"][rank:]
    x_dbl[96:96 + rank] = m["W_x"][:rank]
    dt_proj = np.zeros((C, INNER), np.float32)
    dt_proj[96:96 + rank] = m["W_dt"].T
    directions = "durl"
    m_phi = np.stack([i["L1_ffn_M_phi_plus"], i["L1_ffn_M_phi_minus"]], 1)
    arrays = {
        "x": i["x"].reshape(IMG, C, LEN).transpose(1, 0, 2).reshape(C, TOK),
        "ident": np.eye(C, dtype=np.float32), "mean": np.full((C, C), 1 / C, np.float32),
        "order": order, "select": select, "less": less, "mask": mask,
        "in": m["W_in"].T, "x_proj": by_half(x_dbl.T), "dt_proj": dt_proj, "out_proj": by_half(m["W_out"].T),
        "gamma": m["gamma"][:, None], "beta": m["beta"][:, None],
        "columns": np.concatenate([
            m["gamma"][:, None], m["beta"][:, None], by_half(m["conv_b"]), by_half(m["b_dt"]), by_half(m["D_skip"]),
            over_partitions(np.concatenate([m["s1"], m["s2"]]))], 1),
        "a_log": by_half(m["A_log"]), "conv_w": over_partitions(m["conv_w"][:, 0].T),
        "w_p": m["W_p"].T, "b_p": m["b_p"][:, None],
        "router": i["L0_ffn_router_w"], "expert": i["L0_ffn_expert_w"].transpose(1, 0, 2),
        "bias": i["L0_ffn_expert_b"],
        "router_b": over_partitions(np.broadcast_to(i["L0_ffn_router_b"], (SUB, EXPERTS))),
        "index": over_partitions(np.arange(EXPERTS, dtype=np.float32)),
        "sweep": np.stack([i["L1_conv_w_" + d] for d in directions]).transpose(2, 0, 3, 1),
        "sweep_b": np.stack([i["L1_conv_b_" + d] for d in directions], 1),
        "log_weights": over_partitions(i["L1_ffn_log_weights"]), "gumbel": over_partitions(i["L1_ffn_gumbel"]),
        "sigma": np.tile(i["L1_ffn_sigma"], C // FILTERS)[:, None], "segment_of": segment_of,
        "m_u_all": i["L1_ffn_M_u"].transpose(2, 0, 1, 3),
        "m_all": m_phi.swapaxes(3, 4).reshape(C, C * C), "branch_of": branch_of, "filter_of": filter_of,
        "phi": i["L1_ffn_phi"].reshape(BLOCKS, 128, FILTERS).swapaxes(1, 2), "alternate": alternate,
        "dft": dft.reshape(C, 2, C), "inverse": inverse.reshape(C, 64), "dft_taps": planes.astype(np.float32),
        "forward": forward, "backward": backward,
    }
    nc = bacc.Bacc("TRN2", target_bir_lowering=False, num_devices=1, dynamic_dma_scratch_size=1024)
    arrays = {f"in_{k}": np.ascontiguousarray(v) for k, v in arrays.items()}
    args = {k[3:]: nc.dram_tensor(k, v.shape, mybir.dt.from_np(v.dtype), kind="ExternalInput").ap()
            for k, v in arrays.items()}
    out = nc.dram_tensor("out", (C, TOK), F32, kind="ExternalOutput").ap()
    metaformer(nc, args, out)
    result = run_bass_kernel_spmd(nc, [arrays], core_ids=[0]).results[0]["out"]
    return np.ascontiguousarray(result.reshape(C, IMG, LEN).transpose(1, 0, 2)).reshape(IMG, C, SIDE, SIDE)
```
